# Optimizing a Trainium2 kernel written in Bass

```python
import numpy as np
import jax
import jax.numpy as jnp

def _softmax(x, axis=-1):
    return jax.nn.softmax(x, axis=axis)

def _gelu(x):
    return jax.nn.gelu(x, approximate=True)

def _silu(x):
    return jax.nn.silu(x)

def _sigmoid(x):
    return jax.nn.sigmoid(x)

def _layernorm(x, axis=-1, eps=1e-05):
    m = jnp.mean(x, axis=axis, keepdims=True)
    v = jnp.var(x, axis=axis, keepdims=True)
    return (x - m) / jnp.sqrt(v + eps)

def _scatter_add(tgt, idx, src, axis=0):
    return tgt.at[idx].add(src)

def _segment_sum(src, seg, n):
    return jax.ops.segment_sum(src, seg, n)
kernel_name = 'mk_conv_preact_d2_conv_nchw768_r2_e7c208'

def setup_inputs(seed: int=0):
    np.random.seed(seed)
    _w = jnp.asarray

    def _rec_inputs():
        import jax
        import jax.numpy as jnp
        _gk = jax.random.key(seed)
        x = -4.65e-05 + 0.9999 * jax.random.normal(jax.random.fold_in(_gk, 1), (16, 384, 32, 32), jnp.float32)
        return x
    x = _rec_inputs()

    def _L0_conv_setup():
        import jax, jax.numpy as jnp
        from jax import lax
        import numpy as np
        H = W = 32
        SCALE = 64.0
        STRIDE = 16
        CHAN_PER_POS = 16
        KSIZE = 3
        SIGMA = 0.5
        BATCH = 16

        def _init_offset_grid():
            offs = []
            n = 3
            for ih in range(-n, n + 1):
                for iw in range(-n, n + 1):
                    if ih == 0 and iw == 0:
                        continue
                    offs.append([iw * STRIDE / SCALE, ih * STRIDE / SCALE])
            return np.array(offs, dtype=np.float32)

        def _displace(x, offset):
            B, C, h, w = x.shape
            F_off = offset.shape[0]
            bind = C // F_off
            off_px = offset * SCALE
            off_int = lax.stop_gradient(jnp.round(off_px))
            sub = off_px - off_int
            dx = jnp.repeat(off_int[:, 0].astype(jnp.int32), bind)
            dy = jnp.repeat(off_int[:, 1].astype(jnp.int32), bind)
            iy = jnp.arange(h)[None, :] - dy[:, None]
            ix = jnp.arange(w)[None, :] - dx[:, None]
            vy = (iy >= 0) & (iy < h)
            vx = (ix >= 0) & (ix < w)
            iyc = jnp.clip(iy, 0, h - 1)
            ixc = jnp.clip(ix, 0, w - 1)
            ch = jnp.arange(C)
            shifted = x[:, ch[:, None, None], iyc[:, :, None], ixc[:, None, :]]
            mask = (vy[:, :, None] & vx[:, None, :]).astype(x.dtype)
            shifted = shifted * mask[None]
            r = jnp.arange(KSIZE, dtype=x.dtype) - KSIZE // 2
            fx = r[None, :]
            fy = r[:, None]
            kx = fx[None] + sub[:, 0][:, None, None]
            ky = fy[None] + sub[:, 1][:, None, None]
            kern = jnp.exp(-(kx * kx + ky * ky) / (2.0 * SIGMA * SIGMA))
            kern = kern / kern.sum(axis=(1, 2), keepdims=True)
            kern_c = jnp.repeat(kern, bind, axis=0)
            out = lax.conv_general_dilated(shifted, kern_c[:, None, :, :], window_strides=(1, 1), padding='SAME', feature_group_count=C, dimension_numbers=('NCHW', 'OIHW', 'NCHW'))
            return out
        key = jax.random.key(seed)
        k1, k2 = jax.random.split(key)
        C = 48 * CHAN_PER_POS
        x = jax.random.normal(k1, (BATCH, C, H, W), dtype=jnp.float32)
        offset = jnp.asarray(_init_offset_grid()) + 0.01 * jax.random.normal(k2, (48, 2), dtype=jnp.float32)
        return {'x': x, 'offset': offset}
    _L0_conv_all = _L0_conv_setup()
    _L0_conv_in = {k: v for k, v in _L0_conv_all.items() if k in ('offset',)}
    del _L0_conv_all

    def _L1_conv_setup():
        import math
        import jax, jax.numpy as jnp
        import numpy as np
        DIM = 384
        TARGET_DIM = 512

        def _hadamard_matrix(n: int) -> np.ndarray:
            H = np.array([[1.0]], dtype=np.float32)
            while H.shape[0] < n:
                H = np.block([[H, H], [H, -H]])
            return H / math.sqrt(n)
        _H = jnp.asarray(_hadamard_matrix(TARGET_DIM))
        key = jax.random.key(seed)
        x = jax.random.normal(key, (16, 384, 56, 56), dtype=jnp.float32)
        return {'x': x}
    _L1_conv_all = _L1_conv_setup()
    _L1_conv_in = {k: v for k, v in _L1_conv_all.items() if k in ()}
    del _L1_conv_all
    return {'x': x, 'L0_conv_offset': _L0_conv_in['offset']}

def reference(x, L0_conv_offset):
    import jax
    import jax.numpy as jnp

    def _L0_conv_ref(x, offset):
        import jax, jax.numpy as jnp
        from jax import lax
        import numpy as np
        H = W = 32
        SCALE = 64.0
        STRIDE = 16
        CHAN_PER_POS = 16
        KSIZE = 3
        SIGMA = 0.5
        BATCH = 16

        def _init_offset_grid():
            offs = []
            n = 3
            for ih in range(-n, n + 1):
                for iw in range(-n, n + 1):
                    if ih == 0 and iw == 0:
                        continue
                    offs.append([iw * STRIDE / SCALE, ih * STRIDE / SCALE])
            return np.array(offs, dtype=np.float32)

        def _displace(x, offset):
            B, C, h, w = x.shape
            F_off = offset.shape[0]
            bind = C // F_off
            off_px = offset * SCALE
            off_int = lax.stop_gradient(jnp.round(off_px))
            sub = off_px - off_int
            dx = jnp.repeat(off_int[:, 0].astype(jnp.int32), bind)
            dy = jnp.repeat(off_int[:, 1].astype(jnp.int32), bind)
            iy = jnp.arange(h)[None, :] - dy[:, None]
            ix = jnp.arange(w)[None, :] - dx[:, None]
            vy = (iy >= 0) & (iy < h)
            vx = (ix >= 0) & (ix < w)
            iyc = jnp.clip(iy, 0, h - 1)
            ixc = jnp.clip(ix, 0, w - 1)
            ch = jnp.arange(C)
            shifted = x[:, ch[:, None, None], iyc[:, :, None], ixc[:, None, :]]
            mask = (vy[:, :, None] & vx[:, None, :]).astype(x.dtype)
            shifted = shifted * mask[None]
            r = jnp.arange(KSIZE, dtype=x.dtype) - KSIZE // 2
            fx = r[None, :]
            fy = r[:, None]
            kx = fx[None] + sub[:, 0][:, None, None]
            ky = fy[None] + sub[:, 1][:, None, None]
            kern = jnp.exp(-(kx * kx + ky * ky) / (2.0 * SIGMA * SIGMA))
            kern = kern / kern.sum(axis=(1, 2), keepdims=True)
            kern_c = jnp.repeat(kern, bind, axis=0)
            out = lax.conv_general_dilated(shifted, kern_c[:, None, :, :], window_strides=(1, 1), padding='SAME', feature_group_count=C, dimension_numbers=('NCHW', 'OIHW', 'NCHW'))
            return out
        return _displace(x, offset)

    def _L1_conv_ref(x):
        import math
        import jax, jax.numpy as jnp
        import numpy as np
        DIM = 384
        TARGET_DIM = 512

        def _hadamard_matrix(n: int) -> np.ndarray:
            H = np.array([[1.0]], dtype=np.float32)
            while H.shape[0] < n:
                H = np.block([[H, H], [H, -H]])
            return H / math.sqrt(n)
        _H = jnp.asarray(_hadamard_matrix(TARGET_DIM))
        B, C, Hs, Ws = x.shape
        xr = jnp.transpose(x, (0, 2, 3, 1)).reshape(-1, DIM)
        xp = jnp.pad(xr, ((0, 0), (0, TARGET_DIM - DIM)))
        y = xp @ _H.astype(x.dtype)
        y = y[:, :DIM]
        y = y.reshape(B, Hs, Ws, C)
        return jnp.transpose(y, (0, 3, 1, 2))

    def _gn(v, G=32, eps=1e-05):
        B_, C_, H_, W_ = v.shape
        g = v.reshape(B_, G, C_ // G, H_, W_)
        m = jnp.mean(g, axis=(2, 3, 4), keepdims=True)
        s = jnp.var(g, axis=(2, 3, 4), keepdims=True)
        return ((g - m) / jnp.sqrt(s + eps)).reshape(v.shape)

    def _ln_c(v, eps=1e-06):
        m = jnp.mean(v, axis=1, keepdims=True)
        s = jnp.var(v, axis=1, keepdims=True)
        return (v - m) / jnp.sqrt(s + eps)

    def _ln_t(v, eps=1e-05):
        m = jnp.mean(v, axis=-1, keepdims=True)
        s = jnp.var(v, axis=-1, keepdims=True)
        return (v - m) / jnp.sqrt(s + eps)

    def _to_tokens(v):
        B_, C_, H_, W_ = v.shape
        return v.reshape(B_, C_, H_ * W_).transpose(0, 2, 1)

    def _from_tokens(t, like):
        B_, C_, H_, W_ = like.shape
        return t.transpose(0, 2, 1).reshape(B_, C_, H_, W_)
    x = x + _L0_conv_ref(_gn(x), L0_conv_offset)
    x = x + _L1_conv_ref(_gn(x))
    return x

_drawn_inputs = setup_inputs


def setup_inputs(seed=0):
    import zlib

    import numpy as np

    out = dict(_drawn_inputs(seed))
    spreads = {}
    factors = {}
    for name, (base, spread) in spreads.items():
        noise = np.random.default_rng([zlib.crc32(name.encode()), seed]).standard_normal(out[name].shape)
        drawn = base * np.exp(spread * noise) if base else spread * noise
        out[name] = jnp.asarray(drawn.astype(out[name].dtype))
    for name, factor in factors.items():
        out[name] = (out[name] * factor).astype(out[name].dtype)
    return out
```

```python
import numpy as np
import concourse.bass as bass
from concourse import mybir
from contextlib import ExitStack

FP32 = mybir.dt.float32
FP16 = mybir.dt.float16
INT32 = mybir.dt.int32
ALU = mybir.AluOpType
ACT = mybir.ActivationFunctionType
AX = mybir.AxisListType

BATCH, CHANNELS, HEIGHT, WIDTH = 16, 384, 32, 32
PIXELS = HEIGHT * WIDTH
OFFSETS = 48
BIND = CHANNELS // OFFSETS
PX_SCALE = 64.0
CT = CHANNELS // 128
FPT = 128 // BIND
GROUP = CHANNELS // 32
EPS = 1e-5
TARGET = 512
ROUND = 12582912.0
FAR = 31.5
HALF_SCALE = 256.0

RING = 12
EXTRA = BATCH - RING
DEEP = 3
FAST = 9
TAPS_X, TAPS_Y = WIDTH, 6
MORE_LINKS = 33
CHUNKS = 8

LOT = 4
LOTS = [(i, i + LOT) for i in range(EXTRA, BATCH + EXTRA, LOT)]
QUADS = BATCH // LOT

G_IOTA, G_DX, G_DY, G_NEAR = 0, 48, 83, 92
G_ROW = G_NEAR + 44
G_COL = G_ROW + CHUNKS
G_EYE = G_COL + 1
G_SUM = G_EYE + 128
SUM_BLOCKS = [(t, t2) for t in range(CT) for t2 in range(CT) if abs(t - t2) <= 1]
G_OWN = G_SUM + 128 * len(SUM_BLOCKS)
G_SUB = G_OWN + FPT
G_END = G_SUB + 1


def geometry_constants():
    g = np.zeros((128, G_END), np.float32)
    p = np.arange(128)
    yi, xi = p // WIDTH, p % WIDTH
    g[:, G_IOTA:G_IOTA + OFFSETS] = np.arange(OFFSETS)
    g[:, G_DX:G_DX + 32] = xi[:, None] - np.arange(32)[None]
    g[:, G_DX + 32:G_DX + 35] = [-1, 0, 1]
    g[:, G_DY:G_DY + 6] = yi[:, None] - np.arange(6)[None] + 1
    g[:, G_DY + 6:G_DY + 9] = [-1, 0, 1]
    g[:, G_NEAR:G_NEAR + 44] = np.abs(g[:, G_DX:G_DX + 44]) <= 1
    g[:, G_ROW:G_ROW + CHUNKS] = 4 * np.arange(CHUNKS)[None] + yi[:, None]
    g[:, G_COL] = xi
    g[:, G_EYE:G_EYE + 128] = np.eye(128)
    for n, (t, t2) in enumerate(SUM_BLOCKS):
        same = (128 * t + p)[:, None] // GROUP == (128 * t2 + p)[None] // GROUP
        g[:, G_SUM + 128 * n:G_SUM + 128 * (n + 1)] = same
    g[:, G_OWN:G_OWN + FPT] = p[:, None] // BIND == np.arange(FPT)[None]
    g[:, G_SUB] = p % BIND
    return g


def hadamard_constants():
    h = np.array([[1.0]], np.float32)
    while h.shape[0] < 128:
        h = np.block([[h, h], [h, -h]])
    return np.concatenate([h, -h], axis=1).astype(np.float16)


def sign_block(t, m):
    return bin(t & m).count("1") % 2


def blocks_in(u):
    return (FAST - u + DEEP - 1) // DEEP


def build(nc, x_pad, offset, geo, had, out):
    ds = bass.ds
    x1_rows = nc.dram_tensor("x1_rows", [FAST * BIND, BATCH * PIXELS], FP32).ap()
    stat_rows = nc.dram_tensor("stat_rows", [CHANNELS, BATCH * 2], FP32).ap()
    x1_more = nc.dram_tensor("x1_more", [(OFFSETS - FAST) * BIND, BATCH * PIXELS], FP32).ap()
    gn_rows = nc.dram_tensor("gn_rows", [CHANNELS, BATCH * 2], FP32).ap()
    x_bcp = x_pad[:, PIXELS:PIXELS + CHANNELS * PIXELS].rearrange("b (t c n) -> b c t n", t=CT, c=128)
    out_v = out.rearrange("b (t c) h w -> b c t (h w)", t=CT)
    ctx = ExitStack()
    with ctx:
        def sb(name, shape, dt=FP32):
            return ctx.enter_context(nc.sbuf_tensor(name, shape, dt))

        def sem(name):
            return ctx.enter_context(nc.semaphore(name))

        ring = sb("ring", [128, CT, RING, PIXELS])
        blk = sb("blk", [128, 2 * DEEP, PIXELS])
        parts = sb("parts", [128, 2, 2, CT, PIXELS], FP16)
        geo_sb = sb("geo_sb", [128, G_END])
        had_sb = sb("had_sb", [128, 2, 128], FP16)
        off_sb = sb("off_sb", [128, 2 * OFFSETS])
        px = sb("px", [128, 5, OFFSETS])
        wk = sb("wk", [128, 6, OFFSETS])
        rank = sb("rank", [128, OFFSETS])
        scrap = sb("scrap", [128, 4])
        count_f = sb("count_f", [128, 1])
        count_i = sb("count_i", [128, 1], INT32)
        sel = sb("sel", [128, FAST, 5])
        taps = sb("taps", [128, FAST, 44])
        norm = sb("norm", [128, FAST, 2])
        view = sb("view", [128, FAST, CHUNKS + 1])
        place_f = sb("place_f", [128, FAST, 4])
        place = sb("place", [128, FAST, 4], INT32)
        rows_f = sb("rows_f", [128, 2, QUADS, CT])
        rows = sb("rows", [128, 2, QUADS, CT], INT32)
        halfstat = sb("halfstat", [128, 4, CT, 2, 6])
        stat = sb("stat", [128, CT, BATCH, 2])
        gn = sb("gn", [128, CT, BATCH, 2])
        tmp = sb("tmp", [128, 4, CT, BATCH])
        blk_gn = sb("blk_gn", [128, DEEP, 2])
        blk_half = sb("blk_half", [128, DEEP, 2, 6])
        blk_stat = sb("blk_stat", [128, DEEP, 2])
        early = parts[:, :, :, :, :].rearrange("p a b c d -> p (a b c d)").bitcast(FP32)
        wide = early[:, 0:OFFSETS * OFFSETS]
        flip = early[:, 0:2 * PIXELS].rearrange("p (u j c) -> p u j c", u=2, c=128)
        conv_w = early[:, OFFSETS * OFFSETS:OFFSETS * OFFSETS + FAST * TAPS_Y * TAPS_X]\
            .rearrange("p (k y x) -> p k y x", k=FAST, y=TAPS_Y)

        ps = [ctx.enter_context(nc.psum_tensor(f"ps{n}", [128, 2, 512], FP32)) for n in range(4)]

        load_done = [sem(f"load_done{n}") for n in range(4)]
        const_in = sem("const_in")
        dve_link = sem("dve_link")
        stat_done = sem("stat_done")
        rank_done = sem("rank_done")
        place_done = sem("place_done")
        exp_in = sem("exp_in")
        exp_done = sem("exp_done")
        conv_w_done = sem("conv_w_done")
        sum_in = sem("sum_in")
        sum_done = sem("sum_done")
        std_in = sem("std_in")
        std_done = sem("std_done")
        gn_done = sem("gn_done")
        x_in = [sem(f"x_in{u}") for u in range(DEEP)]
        shift_in = [sem(f"shift_in{u}") for u in range(DEEP)]
        gn_in = [sem(f"gn_in{u}") for u in range(DEEP)]
        centred = sem("centred")
        flipped = sem("flipped")
        flip_masked = sem("flip_masked")
        convolved = sem("convolved")
        x1_done = sem("x1_done")
        blk_stat_done = sem("blk_stat_done")
        blk_out = [sem(f"blk_out{u}") for u in range(DEEP)]
        xn_done = sem("xn_done")
        high_done = sem("high_done")
        low_done = sem("low_done")
        product_done = sem("product_done")
        result_done = sem("result_done")
        store_done = [sem(f"store_done{u}") for u in range(2)]
        reload_done = sem("reload_done")
        patch_done = [sem(f"patch_done{lot}") for lot in range(len(LOTS))]
        stat_patched = sem("stat_patched")
        gn_out = sem("gn_out")
        more_link = sem("more_link")
        more_placed = sem("more_placed")
        more_exp_in = sem("more_exp_in")
        more_exp_done = sem("more_exp_done")
        more_conv_w = sem("more_conv_w")
        more_in = sem("more_in")
        more_centred = sem("more_centred")
        more_flipped = sem("more_flipped")
        more_masked = sem("more_masked")
        more_convolved = sem("more_convolved")
        more_ready = sem("more_ready")
        more_out = sem("more_out")
        more_patched = sem("more_patched")
        block = ctx.enter_context(nc.Block())

        def bc(ap, shape):
            return ap.broadcast_to(shape)

        @block.sync
        def _(sp):
            sp.dma_start(off_sb[:, :], bc(offset.rearrange("(a f) k -> a (f k)", a=1), [128, 2 * OFFSETS])).then_inc(const_in, 16)
            sp.dma_start(geo_sb[:, :], geo).then_inc(const_in, 16)
            sp.dma_start(had_sb[:, :, :], had.rearrange("p (s n) -> p s n", s=2)).then_inc(const_in, 16)
            for i in range(BATCH):
                if i >= 4:
                    sp.wait_ge(load_done[i % 4], 16 * (i // 4))
                if i >= RING:
                    sp.wait_ge(stat_done, i - RING + 1)
                sp.dma_start(ring[:, :, i % RING, :], x_bcp[i]).then_inc(load_done[i % 4], 16)

            def fetch(k, u, turn):
                x_at = sp.value_load(place[0:1, k, 2:3], min_val=PIXELS, max_val=PIXELS * (CHANNELS - BIND + 1))
                s_at = sp.value_load(place[0:1, k, 3:4], min_val=1, max_val=PIXELS * (CHANNELS - BIND + 2) - 1)
                if turn > 0:
                    sp.wait_ge(blk_out[u], 32 * turn)
                sp.dma_start(blk[:, u, :],
                             x_pad[:, ds(x_at, BIND * PIXELS)].rearrange("b (c n) -> b c n", c=BIND)).then_inc(x_in[u], 16)
                sp.dma_start(blk[:, DEEP + u, :],
                             x_pad[:, ds(s_at, BIND * PIXELS)].rearrange("b (c n) -> b c n", c=BIND)).then_inc(shift_in[u], 16)

            def fetch_gn(k, u):
                c_at = sp.value_load(place[0:1, k, 0:1], min_val=0, max_val=CHANNELS - BIND)
                sp.dma_start(blk_gn[:, u, :], gn_rows[ds(c_at, BIND), :].rearrange("c (b k) -> b c k", k=2)).then_inc(gn_in[u], 16)

            sp.wait_ge(place_done, 1)
            for k in range(DEEP):
                fetch(k, k, 0)
            sp.wait_ge(gn_done, 1)
            sp.dma_start(gn_rows.rearrange("(t c) n -> c t n", t=CT), gn[:, :, :, :].rearrange("c t b k -> c t (b k)")).then_inc(gn_out, 16)
            sp.dma_start(stat_rows.rearrange("(t c) n -> c t n", t=CT), stat[:, :, :, :].rearrange("c t b k -> c t (b k)")).then_inc(gn_out, 16)
            sp.wait_ge(gn_out, 32)
            for k in range(FAST):
                if k >= DEEP:
                    fetch(k, k % DEEP, k // DEEP)
                fetch_gn(k, k % DEEP)

            active = sp.value_load(count_i[0:1, 0:1], min_val=0, max_val=OFFSETS)
            with sp.If(active > FAST):
                for u in range(DEEP):
                    sp.wait_ge(blk_out[u], 32 * blocks_in(u))
                with sp.Fori(FAST, OFFSETS) as k:
                    m = k - FAST
                    sp.wait_ge(more_placed, 1)
                    sp.sem_clear(more_placed)
                    c_at = sp.value_load(place[0:1, 0, 0:1], min_val=0, max_val=CHANNELS - BIND)
                    x_at = sp.value_load(place[0:1, 0, 2:3], min_val=PIXELS, max_val=PIXELS * (CHANNELS - BIND + 1))
                    s_at = sp.value_load(place[0:1, 0, 3:4], min_val=1, max_val=PIXELS * (CHANNELS - BIND + 2) - 1)
                    sp.dma_start(blk[:, 0, :], x_pad[:, ds(x_at, BIND * PIXELS)].rearrange("b (c n) -> b c n", c=BIND)).then_inc(more_in, 16)
                    sp.dma_start(blk[:, DEEP, :], x_pad[:, ds(s_at, BIND * PIXELS)].rearrange("b (c n) -> b c n", c=BIND)).then_inc(more_in, 16)
                    sp.dma_start(blk_gn[:, 0, :], gn_rows[ds(c_at, BIND), :].rearrange("c (b k) -> b c k", k=2)).then_inc(more_in, 16)
                    sp.wait_ge(more_ready, m + 1)
                    sp.dma_start(x1_more[ds(m * BIND, BIND), :].rearrange("c (b n) -> b c n", b=BATCH), blk[:, 0, :]).then_inc(more_out, 16)
                    sp.dma_start(stat_rows[ds(c_at, BIND), :].rearrange("c (b k) -> b c k", k=2), blk_stat[:, 0, :]).then_inc(more_out, 16)

            def store(i):
                n = i - EXTRA
                sp.wait_ge(result_done, CT * (n + 1))
                if n >= 2:
                    sp.wait_ge(store_done[n % 2], 16 * (n // 2))
                sp.dma_start(out_v[i % BATCH], ring[:, :, i % RING, :]).then_inc(store_done[n % 2], 16)

            for i in range(EXTRA, 2 * EXTRA + 2):
                store(i)
            for i in range(BATCH, BATCH + EXTRA):
                sp.dma_start(ring[:, :, i % RING, :], x_bcp[i - BATCH]).then_inc(reload_done, 16)
            for i in range(2 * EXTRA + 2, BATCH + EXTRA):
                store(i)
            for u in range(2):
                sp.wait_ge(store_done[u], 16 * (BATCH // 2))

        @block.gpsimd
        def _(pool):
            pool.wait_ge(rank_done, 1)
            for u in range(DEEP):
                pool.wait_ge(blk_out[u], 32 * blocks_in(u))
            active = pool.value_load(count_i[0:1, 0:1], min_val=0, max_val=OFFSETS)
            with pool.If(active > FAST):
                pool.wait_ge(more_out, 32 * (OFFSETS - FAST))
            pool.dma_start(stat[:, :, :, :].rearrange("p t b k -> p t (b k)"),
                           stat_rows.rearrange("(t c) n -> c t n", t=CT)).then_inc(stat_patched, 16)

            def patch(table, which, lot, first, signal):
                for t in range(CT):
                    pool.indirect_dma_start(
                        ring[:, t, first % RING:first % RING + LOT, :].rearrange("p b n -> p (b n)"), None,
                        table.rearrange("c (q n) -> (c q) n", q=QUADS),
                        bass.IndirectOffsetOnAxis(ap=rows[:, which, (first % BATCH) // LOT, t:t + 1], axis=0),
                        bounds_check=table.shape[0] * QUADS - 1, oob_is_err=False).then_inc(signal, 16)

            for lot, (first, end) in enumerate(LOTS):
                if first == BATCH:
                    pool.wait_ge(reload_done, 16 * EXTRA)
                with pool.If(active > FAST):
                    patch(x1_more, 1, lot, first, more_patched)
                    pool.wait_ge(more_patched, 16 * CT * (lot + 1))
                patch(x1_rows, 0, lot, first, patch_done[lot])

        @block.scalar
        def _(act):
            act.wait_ge(exp_in, 1)
            act.activation(taps[:, :, :], taps[:, :, :], ACT.Exp, scale=-2.0).then_inc(exp_done, 1)
            act.wait_ge(std_in, 1)
            act.activation(tmp[:, 2, :, :], tmp[:, 2, :, :], ACT.Sqrt).then_inc(std_done, 1)

            def centre(k, u):
                act.wait_ge(shift_in[u], 16 * (k // DEEP + 1))
                act.wait_ge(gn_in[u], 16 * (k // DEEP + 1))
                act.activation(blk[:, DEEP + u, :], blk[:, DEEP + u, :], ACT.Identity,
                               bias=blk_gn[:, u, 0:1], scale=1.0).then_inc(centred, 1)

            def leave(k, u):
                c_at = act.value_load(place[0:1, k, 0:1], min_val=0, max_val=CHANNELS - BIND)
                act.wait_ge(x1_done, k + 1)
                act.dma_start(x1_rows[BIND * k:BIND * (k + 1), :].rearrange("c (b n) -> b c n", b=BATCH), blk[:, u, :]).then_inc(blk_out[u], 16)
                act.wait_ge(blk_stat_done, k + 1)
                act.dma_start(stat_rows[ds(c_at, BIND), :].rearrange("c (b k) -> b c k", k=2), blk_stat[:, u, :]).then_inc(blk_out[u], 16)

            for k in range(FAST):
                centre(k, k % DEEP)
                if k >= 2:
                    leave(k - 2, (k - 2) % DEEP)
            for k in range(FAST - 2, FAST):
                leave(k, k % DEEP)

            active = act.value_load(count_i[0:1, 0:1], min_val=0, max_val=OFFSETS)
            with act.If(active > FAST):
                with act.Fori(FAST, OFFSETS) as k:
                    m = k - FAST
                    act.wait_ge(more_exp_in, m + 1)
                    act.activation(taps[:, 0:1, :], taps[:, 0:1, :], ACT.Exp, scale=-2.0).then_inc(more_exp_done, 1)
                    act.wait_ge(more_in, 48 * m + 48)
                    act.activation(blk[:, DEEP, :], blk[:, DEEP, :], ACT.Identity,
                                   bias=blk_gn[:, 0, 0:1], scale=1.0).then_inc(more_centred, 1)

            act.wait_ge(std_in, 2)
            act.activation(tmp[:, 2, :, :], tmp[:, 2, :, :], ACT.Sqrt).then_inc(std_done, 1)
            act.wait_ge(gn_done, 2)

            def split(n, u, turn, i):
                for t in range(CT):
                    act.wait_ge(low_done, CT * (n - 1) + t + 1) if n >= 1 else None
                    act.activation(blk[:, t, :], ring[:, t, i % RING, :], ACT.Identity,
                                   bias=gn[:, t, i % BATCH, 1:2], scale=gn[:, t, i % BATCH, 0:1]).then_inc(xn_done, 1)
                if turn:
                    act.wait_ge(product_done, CT * (n - 1))
                for t in range(CT):
                    act.wait_ge(xn_done, CT * n + t + 1)
                    act.activation(parts[:, u, 0, t, :], blk[:, t, :], ACT.Copy).then_inc(high_done, 1)

            for i in range(EXTRA, BATCH + EXTRA):
                n = i - EXTRA
                for lot, (first, end) in enumerate(LOTS):
                    if i == first:
                        act.wait_ge(patch_done[lot], 16 * CT)
                split(n, n % 2, n // 2, i)

        @block.tensor
        def _(pe):
            pe.wait_ge(const_in, 48)

            def group_sums(turn):
                for step in range(2):
                    pe.wait_ge(sum_in, 2 * turn + step + 1)
                    for t2 in range(CT):
                        pairs = [(n, t) for n, (t, tt) in enumerate(SUM_BLOCKS) if tt == t2]
                        for c, (n, t) in enumerate(pairs):
                            src = stat[:, t, :, 0] if step == 0 else tmp[:, 1, t, :]
                            last = pe.matmul(ps[0][:, step, BATCH * t2:BATCH * (t2 + 1)],
                                             geo_sb[:, G_SUM + 128 * n:G_SUM + 128 * (n + 1)], src,
                                             start=(c == 0), stop=(c == len(pairs) - 1))
                    last.then_inc(sum_done, 1)

            group_sums(0)
            pe.wait_ge(gn_done, 1)
            pe.wait_ge(conv_w_done, 1)

            eye = geo_sb[:, G_EYE:G_EYE + 128]

            def transpose_block(pixels, shifted):
                for j in range(CHUNKS):
                    last = pe.transpose(pixels[:, j // 4, 128 * (j % 4):128 * (j % 4 + 1)],
                                        shifted[:, 128 * j:128 * (j + 1)], eye)
                return last

            def convolve_block(sums, pixels, weights):
                for bank in range(2):
                    seen = 16 * bank
                    for j in range(3 * bank, 3 * bank + 5):
                        lo = max(4 * j - 1, 16 * bank)
                        hi = min(4 * j + 5, 16 * bank + 16)
                        for a, b in ((lo, seen), (seen, hi)):
                            if a < b:
                                last = pe.matmul(sums[:, bank, 32 * (a - 16 * bank):32 * (b - 16 * bank)],
                                                 pixels[:, j, :], weights[:, a - (4 * j - 1):b - (4 * j - 1), :],
                                                 start=(j == 3 * bank), stop=(j == 3 * bank + 4 and b == hi))
                        seen = hi
                return last

            def transposes(k):
                pe.wait_ge(centred, k + 1)
                if k >= 2:
                    pe.wait_ge(flip_masked, k - 1)
                transpose_block(ps[k % 2], blk[:, DEEP + k % DEEP, :]).then_inc(flipped, 1)

            def convolve(k):
                pe.wait_ge(flip_masked, k + 1)
                if k >= 2:
                    pe.wait_ge(x1_done, k - 1)
                convolve_block(ps[2 + k % 2], flip[:, k % 2], conv_w[:, k]).then_inc(convolved, 1)

            transposes(0)
            for k in range(FAST):
                if k + 1 < FAST:
                    transposes(k + 1)
                convolve(k)

            pe.wait_ge(rank_done, 1)
            active = pe.value_load(count_i[0:1, 0:1], min_val=0, max_val=OFFSETS)
            with pe.If(active > FAST):
                pe.wait_ge(x1_done, FAST)
                with pe.Fori(FAST, OFFSETS) as k:
                    m = k - FAST
                    pe.wait_ge(more_centred, m + 1)
                    transpose_block(ps[0], blk[:, DEEP, :]).then_inc(more_flipped, 1)
                    pe.wait_ge(more_masked, m + 1)
                    pe.wait_ge(more_conv_w, m + 1)
                    convolve_block(ps[2], flip[:, 1], conv_w[:, 0]).then_inc(more_convolved, 1)

            group_sums(1)
            for n in range(BATCH):
                u = n % 2
                pe.wait_ge(low_done, CT * (n + 1))
                for m in range(CT):
                    if n >= 1:
                        pe.wait_ge(result_done, CT * (n - 1) + m + 1)
                    for h in range(2):
                        for t in range(CT):
                            for part in range(2):
                                last = pe.matmul(ps[m][:, h, :], had_sb[:, sign_block(t, m), :],
                                                 parts[:, u, part, t, 512 * h:512 * (h + 1)],
                                                 start=(t == 0 and part == 0), stop=(t == CT - 1 and part == 1))
                    last.then_inc(product_done, 1)

        @block.vector
        def _(dve):
            links = [0]

            def link(ins):
                links[0] += 1
                ins.then_inc(dve_link, 1)
                dve.wait_ge(dve_link, links[0])

            dve.wait_ge(const_in, 48)
            iota = geo_sb[:, G_IOTA:G_IOTA + OFFSETS]
            off_v = off_sb[:, :].rearrange("p (f k) -> p k f", k=2)
            o, rnd = wk[:, 0:2, :], px[:, 1:3, :]
            link(dve.tensor_scalar(o, off_v, PX_SCALE, 64.0, ALU.mult, ALU.min))
            link(dve.tensor_scalar(o, o, -64.0, None, ALU.max))
            link(dve.tensor_scalar(wk[:, 2:4, :], o, ROUND, None, ALU.add))
            link(dve.tensor_scalar(rnd, wk[:, 2:4, :], ROUND, None, ALU.subtract))
            link(dve.tensor_tensor(px[:, 3:5, :], o, rnd, ALU.subtract))
            dve.tensor_copy(px[:, 0, :], iota)
            link(dve.tensor_tensor(wk[:, 4:6, :], rnd, rnd, ALU.mult))
            link(dve.tensor_scalar(wk[:, 4:6, :], wk[:, 4:6, :], FAR * FAR, None, ALU.is_lt))
            link(dve.tensor_tensor(wk[:, 0, :], wk[:, 4, :], wk[:, 5, :], ALU.mult))
            link(dve.tensor_reduce(count_f[:, :], wk[:, 0, :], AX.X, ALU.add))
            dve.tensor_copy(count_i[:, :], count_f[:, :])
            link(dve.scalar_tensor_tensor(wk[:, 1, :], wk[:, 0, :], -float(OFFSETS), iota, ALU.mult, ALU.add))
            wide_v = wide.rearrange("p (f g) -> p f g", f=OFFSETS)
            full = [128, OFFSETS, OFFSETS]
            link(dve.tensor_tensor(wide_v, bc(wk[:, 1:2, :], full),
                                   bc(wk[:, 1, :].rearrange("p (f o) -> p f o", o=1), full), ALU.is_lt))
            link(dve.tensor_reduce(rank[:, :], wide_v, AX.X, ALU.add))

            own = bc(geo_sb[:, G_OWN:G_OWN + FPT].rearrange("p (o f) -> p o f", o=1), [128, CT, FPT])
            mine = wk[:, 2, :].rearrange("p (t f) -> p t f", t=CT)
            link(dve.tensor_tensor(mine, rank[:, :].rearrange("p (t f) -> p t f", t=CT), own, ALU.mult))
            link(dve.tensor_reduce(rows_f[:, 0, 0, :], mine, AX.X, ALU.add))
            link(dve.tensor_scalar(rows_f[:, 0, 0, :], rows_f[:, 0, 0, :], float(BIND), geo_sb[:, G_SUB:G_SUB + 1], ALU.mult, ALU.add))
            for q in range(QUADS - 1, -1, -1):
                last = dve.tensor_scalar(rows_f[:, 0, q, :], rows_f[:, 0, 0, :], float(QUADS), float(q), ALU.mult, ALU.add)
            link(last)
            fast_rows = float(FAST * BIND * QUADS)
            link(dve.tensor_scalar(rows_f[:, 1, :, :], rows_f[:, 0, :, :], fast_rows - 0.5, 2.0 * CHANNELS * QUADS, ALU.is_lt, ALU.mult))
            link(dve.tensor_tensor(rows_f[:, 1, :, :], rows_f[:, 1, :, :], rows_f[:, 0, :, :], ALU.add))
            link(dve.tensor_scalar(rows_f[:, 1, :, :], rows_f[:, 1, :, :], fast_rows, None, ALU.subtract))
            dve.tensor_copy(rows[:, :, :, :], rows_f[:, :, :, :]).then_inc(rank_done, 1)

            def slot_parameters(slot_ids, n, link, placed, exp_in, exp_done, exp_count, weighed):
                keep = slice(0, n)
                shape = [128, n, OFFSETS]
                hit = wide[:, 0:n * OFFSETS].rearrange("p (k f) -> p k f", k=n)
                pick = wide[:, n * OFFSETS:2 * n * OFFSETS].rearrange("p (k f) -> p k f", k=n)
                rank_v = rank[:, :].rearrange("p (o f) -> p o f", o=1)
                link(dve.tensor_tensor(hit, bc(rank_v, shape), bc(slot_ids, shape), ALU.is_equal))
                for v in range(5):
                    link(dve.tensor_tensor(pick, hit, bc(px[:, v:v + 1, :], shape), ALU.mult))
                    link(dve.tensor_reduce(sel[:, keep, v], pick, AX.X, ALU.add))
                f, dx, dy = sel[:, keep, 0:1], sel[:, keep, 1:2], sel[:, keep, 2:3]
                link(dve.tensor_scalar(place_f[:, keep, 0:1], f, float(BIND), None, ALU.mult))
                link(dve.tensor_scalar(place_f[:, keep, 1:2], f, 0.0, None, ALU.mult))
                link(dve.tensor_scalar(place_f[:, keep, 2:3], f, float(BIND * PIXELS), float(PIXELS), ALU.mult, ALU.add))
                link(dve.scalar_tensor_tensor(place_f[:, keep, 3:4], dy, -float(WIDTH), dx, ALU.mult, ALU.subtract))
                link(dve.tensor_tensor(place_f[:, keep, 3:4], place_f[:, keep, 3:4], place_f[:, keep, 2:3], ALU.add))
                dve.tensor_copy(place[:, keep, :], place_f[:, keep, :]).then_inc(placed, 1)
                link(dve.tensor_tensor(taps[:, keep, 0:35], bc(geo_sb[:, G_DX:G_DX + 35].rearrange("p (o d) -> p o d", o=1), [128, n, 35]),
                                       bc(sel[:, keep, 3:4], [128, n, 35]), ALU.add))
                link(dve.tensor_tensor(taps[:, keep, 35:44], bc(geo_sb[:, G_DY:G_DY + 9].rearrange("p (o d) -> p o d", o=1), [128, n, 9]),
                                       bc(sel[:, keep, 4:5], [128, n, 9]), ALU.add))
                dve.tensor_tensor(taps[:, keep, :], taps[:, keep, :], taps[:, keep, :], ALU.mult).then_inc(exp_in, 1)
                link(dve.tensor_tensor(view[:, keep, 0:CHUNKS], bc(geo_sb[:, G_ROW:G_ROW + CHUNKS].rearrange("p (o d) -> p o d", o=1), [128, n, CHUNKS]),
                                       bc(dy, [128, n, CHUNKS]), ALU.subtract))
                link(dve.tensor_tensor(view[:, keep, CHUNKS:], bc(geo_sb[:, G_COL:G_COL + 1].rearrange("p (o d) -> p o d", o=1), [128, n, 1]),
                                       dx, ALU.subtract))
                link(dve.tensor_scalar(view[:, keep, :], view[:, keep, :], 15.5, None, ALU.subtract))
                link(dve.tensor_tensor(view[:, keep, :], view[:, keep, :], view[:, keep, :], ALU.mult))
                link(dve.tensor_scalar(view[:, keep, :], view[:, keep, :], 256.0, None, ALU.is_lt))
                link(dve.tensor_tensor(view[:, keep, 0:CHUNKS], view[:, keep, 0:CHUNKS], bc(view[:, keep, CHUNKS:], [128, n, CHUNKS]), ALU.mult))
                dve.wait_ge(exp_done, exp_count)
                link(dve.tensor_tensor(taps[:, keep, :], taps[:, keep, :],
                                       bc(geo_sb[:, G_NEAR:G_NEAR + 44].rearrange("p (o d) -> p o d", o=1), [128, n, 44]), ALU.mult))
                link(dve.tensor_reduce(norm[:, keep, 0:1], taps[:, keep, 32:35], AX.X, ALU.add))
                link(dve.tensor_reduce(norm[:, keep, 1:2], taps[:, keep, 41:44], AX.X, ALU.add))
                link(dve.reciprocal(norm[:, keep, :], norm[:, keep, :]))
                link(dve.tensor_tensor(taps[:, keep, 0:32], taps[:, keep, 0:32], bc(norm[:, keep, 0:1], [128, n, 32]), ALU.mult))
                link(dve.tensor_tensor(taps[:, keep, 35:41], taps[:, keep, 35:41], bc(norm[:, keep, 1:2], [128, n, 6]), ALU.mult))
                link(dve.tensor_tensor(conv_w[:, keep, :, :],
                                       bc(taps[:, keep, 35:41].rearrange("p k (y o) -> p k y o", o=1), [128, n, 6, 32]),
                                       bc(taps[:, keep, 0:32].rearrange("p k (o x) -> p k o x", o=1), [128, n, 6, 32]), ALU.mult))
                dve.tensor_copy(norm[:, keep, :], norm[:, keep, :]).then_inc(weighed, 1)

            def slot_ids(k, n):
                return geo_sb[:, ds(G_IOTA + k, n)].rearrange("p (k o) -> p k o", o=1)

            slot_parameters(slot_ids(0, FAST), FAST, link, place_done, exp_in, exp_done, 1, conv_w_done)

            for i in range(BATCH):
                dve.wait_ge(load_done[i % 4], 16 * (i // 4 + 1))
                for t in range(CT):
                    for h in range(2):
                        last = dve.bn_stats(halfstat[:, i % 4, t, h, :], ring[:, t, i % RING, 512 * h:512 * (h + 1)])
                last.then_inc(stat_done, 1)
                if i % 4 == 3:
                    dve.wait_ge(stat_done, i + 1)
                    for j in range(4):
                        for t in range(CT):
                            last = dve.bn_aggr(stat[:, t, i - 3 + j, :], halfstat[:, j, t, :, :].rearrange("p h s -> p (h s)"))
                    link(last)

            def groupnorm(turn, second):
                mean = stat[:, :, :, 0]
                var = stat[:, :, :, 1]
                dve.memset(scrap[:, 0:1], 0.0).then_inc(sum_in, 1)
                dve.wait_ge(sum_done, 2 * turn + 1)
                flat = lambda a: a.rearrange("p t b -> p (t b)")
                link(dve.tensor_scalar(flat(tmp[:, 0, :, :]), ps[0][:, 0, 0:CT * BATCH], 1.0 / GROUP, None, ALU.mult))
                link(dve.tensor_tensor(tmp[:, 1, :, :], mean, tmp[:, 0, :, :], ALU.subtract))
                link(dve.tensor_tensor(tmp[:, 1, :, :], tmp[:, 1, :, :], tmp[:, 1, :, :], ALU.mult))
                dve.tensor_tensor(tmp[:, 1, :, :], tmp[:, 1, :, :], var, ALU.add).then_inc(sum_in, 1)
                dve.wait_ge(sum_done, 2 * turn + 2)
                dve.tensor_scalar(flat(tmp[:, 2, :, :]), ps[0][:, 1, 0:CT * BATCH], 1.0 / GROUP, EPS, ALU.mult, ALU.add).then_inc(std_in, 1)
                dve.wait_ge(std_done, turn + 1)
                link(dve.reciprocal(tmp[:, 3, :, :], tmp[:, 2, :, :]))
                if not second:
                    dve.tensor_scalar(gn[:, :, :, 0], tmp[:, 0, :, :], -1.0, None, ALU.mult)
                    link(dve.tensor_copy(gn[:, :, :, 1], tmp[:, 3, :, :]))
                else:
                    link(dve.tensor_scalar(gn[:, :, :, 0], tmp[:, 3, :, :], HALF_SCALE, None, ALU.mult))
                    link(dve.scalar_tensor_tensor(gn[:, :, :, 1], tmp[:, 0, :, :], -1.0, gn[:, :, :, 0], ALU.mult, ALU.mult))
                dve.memset(scrap[:, 1:2], 0.0).then_inc(gn_done, 1)

            groupnorm(0, False)

            def mask_pixels(pixels, shifted, k):
                return dve.tensor_tensor(pixels, shifted[:, :, :].rearrange("p a (j c) -> p (a j) c", c=128),
                                         bc(view[:, k, 0:CHUNKS].rearrange("p (j o) -> p j o", o=1), [128, CHUNKS, 128]), ALU.mult)

            def add_displaced(x1, sums, rstd):
                return dve.scalar_tensor_tensor(x1, sums[:, :, :].rearrange("p a n -> p (a n)"), rstd, x1, ALU.mult, ALU.add)

            def mask_block(k):
                dve.wait_ge(flipped, k + 1)
                if k >= 2:
                    dve.wait_ge(convolved, k - 1)
                mask_pixels(flip[:, k % 2], ps[k % 2], k).then_inc(flip_masked, 1)

            def add_block(k):
                u = k % DEEP
                dve.wait_ge(convolved, k + 1)
                dve.wait_ge(x_in[u], 16 * (k // DEEP + 1))
                add_displaced(blk[:, u, :], ps[2 + k % 2], blk_gn[:, u, 1:2]).then_inc(x1_done, 1)
                dve.wait_ge(x1_done, k + 1)
                for h in range(2):
                    last = dve.bn_stats(blk_half[:, u, h, :], blk[:, u, 512 * h:512 * (h + 1)])
                link(last)
                dve.bn_aggr(blk_stat[:, u, :], blk_half[:, u, :, :].rearrange("p h s -> p (h s)")).then_inc(blk_stat_done, 1)

            mask_block(0)
            for k in range(FAST):
                if k + 1 < FAST:
                    mask_block(k + 1)
                add_block(k)

            active = dve.value_load(count_i[0:1, 0:1], min_val=0, max_val=OFFSETS)
            with dve.If(active > FAST):
                dve.wait_ge(convolved, FAST)
                for u in range(DEEP):
                    dve.wait_ge(blk_out[u], 32 * blocks_in(u))
                with dve.Fori(FAST, OFFSETS) as k:
                    m = k - FAST
                    step = [0]

                    def more(ins):
                        step[0] += 1
                        ins.then_inc(more_link, 1)
                        dve.wait_ge(more_link, MORE_LINKS * m + step[0])

                    slot_parameters(slot_ids(k, 1), 1, more, more_placed, more_exp_in, more_exp_done, m + 1, more_conv_w)
                    dve.wait_ge(more_flipped, m + 1)
                    mask_pixels(flip[:, 1], ps[0], 0).then_inc(more_masked, 1)
                    dve.wait_ge(more_convolved, m + 1)
                    more(add_displaced(blk[:, 0, :], ps[2], blk_gn[:, 0, 1:2]))
                    for h in range(2):
                        last = dve.bn_stats(blk_half[:, 0, h, :], blk[:, 0, 512 * h:512 * (h + 1)])
                    more(last)
                    dve.memset(scrap[:, 2:3], 0.0)
                    dve.bn_aggr(blk_stat[:, 0, :], blk_half[:, 0, :, :].rearrange("p h s -> p (h s)")).then_inc(more_ready, 1)
                    dve.wait_ge(more_out, 32 * m + 32)
                    dve.memset(scrap[:, 3:4], 0.0)
                    assert step[0] == MORE_LINKS, step[0]

            dve.wait_ge(stat_patched, 16)
            groupnorm(1, True)

            def result(n, m):
                i = n + EXTRA
                dve.wait_ge(product_done, CT * n + m + 1)
                dve.scalar_tensor_tensor(ring[:, m, i % RING, :], ps[m][:, :, :].rearrange("p a n -> p (a n)"),
                                         1.0 / (HALF_SCALE * float(np.sqrt(TARGET))), ring[:, m, i % RING, :],
                                         ALU.mult, ALU.add).then_inc(result_done, 1)

            for n in range(BATCH):
                u = n % 2
                for t in range(CT):
                    dve.wait_ge(high_done, CT * n + t + 1)
                    if n >= 2:
                        dve.wait_ge(product_done, CT * (n - 1))
                    dve.tensor_tensor(parts[:, u, 1, t, :], blk[:, t, :], parts[:, u, 0, t, :], ALU.subtract).then_inc(low_done, 1)
                    if n >= 1:
                        result(n - 1, t)
            for m in range(CT):
                result(BATCH - 1, m)


def kernel(x, L0_conv_offset):
    import concourse.bacc as bacc
    from concourse.bass_utils import run_bass_kernel_spmd

    x = np.ascontiguousarray(x)
    x_pad = np.zeros((BATCH, (CHANNELS + 2) * PIXELS), x.dtype)
    x_pad[:, PIXELS:PIXELS * (CHANNELS + 1)] = x.reshape(BATCH, -1)
    arrays = {"x_pad": x_pad, "offset": np.ascontiguousarray(L0_conv_offset),
              "geo": geometry_constants(), "had": hadamard_constants()}
    nc = bacc.Bacc("TRN2", target_bir_lowering=False, num_devices=1)
    args = [nc.dram_tensor(name, a.shape, mybir.dt.from_np(a.dtype), kind="ExternalInput").ap() for name, a in arrays.items()]
    out = nc.dram_tensor("out", (BATCH, CHANNELS, HEIGHT, WIDTH), FP32, kind="ExternalOutput").ap()
    build(nc, *args, out)
    r = run_bass_kernel_spmd(nc, [arrays], core_ids=[0])
    return r.results[0]["out"]
```

```python
import numpy as np
import concourse.bass as bass
from concourse import mybir
from contextlib import ExitStack

FP32 = mybir.dt.float32
FP16 = mybir.dt.float16
INT32 = mybir.dt.int32
ALU = mybir.AluOpType
ACT = mybir.ActivationFunctionType
AX = mybir.AxisListType

BATCH, CHANNELS, HEIGHT, WIDTH = 16, 384, 32, 32
PIXELS = HEIGHT * WIDTH
OFFSETS = 48
BIND = CHANNELS // OFFSETS
PX_SCALE = 64.0
CT = CHANNELS // 128
GROUP = CHANNELS // 32
EPS = 1e-5
TARGET = 512
ROUND = 12582912.0
FAR = 31.5
HALF_SCALE = 256.0

RING = 12
EXTRA = BATCH - RING
DEEP = 3
FAST = 9
TAPS_X, TAPS_Y = WIDTH, 6
MORE_LINKS = 33
CHUNKS = 8

LOT = 2
LOTS = [(i, i + LOT) for i in range(EXTRA, BATCH + EXTRA, LOT)]
ROW_LOTS = BATCH // LOT

G_IOTA, G_DX, G_DY, G_NEAR = 0, 48, 83, 92
G_ROW = G_NEAR + 44
G_COL = G_ROW + CHUNKS
G_EYE = G_COL + 1
G_SUM = G_EYE + 128
G_OWN = G_SUM + 128
G_SUB = G_OWN + CT * OFFSETS
G_END = G_SUB + CT


def geometry_constants():
    g = np.zeros((128, G_END), np.float32)
    p = np.arange(128)
    yi, xi = p // WIDTH, p % WIDTH
    g[:, G_IOTA:G_IOTA + OFFSETS] = np.arange(OFFSETS)
    g[:, G_DX:G_DX + 32] = xi[:, None] - np.arange(32)[None]
    g[:, G_DX + 32:G_DX + 35] = [-1, 0, 1]
    g[:, G_DY:G_DY + 6] = yi[:, None] - np.arange(6)[None] + 1
    g[:, G_DY + 6:G_DY + 9] = [-1, 0, 1]
    g[:, G_NEAR:G_NEAR + 44] = np.abs(g[:, G_DX:G_DX + 44]) <= 1
    g[:, G_ROW:G_ROW + CHUNKS] = 4 * np.arange(CHUNKS)[None] + yi[:, None]
    g[:, G_COL] = xi
    g[:, G_EYE:G_EYE + 128] = np.eye(128)
    per_group = GROUP // CT
    g[:, G_SUM:G_SUM + 128] = p[:, None] // per_group == p[None] // per_group
    channel = CT * p[:, None] + np.arange(CT)[None]
    own = channel[:, :, None] // BIND == np.arange(OFFSETS)
    g[:, G_OWN:G_OWN + CT * OFFSETS] = own.reshape(128, -1)
    g[:, G_SUB:G_SUB + CT] = channel % BIND
    return g


def hadamard_constants():
    h = np.array([[1.0]], np.float32)
    while h.shape[0] < TARGET:
        h = np.block([[h, h], [h, -h]])
    h = h[:CHANNELS, :CHANNELS].reshape(128, CT, 128, CT).transpose(0, 1, 3, 2)
    return h.reshape(128, -1).astype(np.float16)


def blocks_in(u):
    return (FAST - u + DEEP - 1) // DEEP


def build(nc, x_pad, offset, geo, had, out):
    ds = bass.ds
    x1_rows = nc.dram_tensor("x1_rows", [FAST * BIND, BATCH * PIXELS], FP32).ap()
    stat_rows = nc.dram_tensor("stat_rows", [CHANNELS, BATCH * 2], FP32).ap()
    x1_more = nc.dram_tensor("x1_more", [(OFFSETS - FAST) * BIND, BATCH * PIXELS], FP32).ap()
    gn_rows = nc.dram_tensor("gn_rows", [CHANNELS, BATCH * 2], FP32).ap()
    x_bcp = x_pad[:, PIXELS:PIXELS + CHANNELS * PIXELS].rearrange("b (c t n) -> b c t n", t=CT, c=128)
    out_v = out.rearrange("b (c t) h w -> b c t (h w)", t=CT)
    ctx = ExitStack()
    with ctx:
        def sb(name, shape, dt=FP32):
            return ctx.enter_context(nc.sbuf_tensor(name, shape, dt))

        def sem(name):
            return ctx.enter_context(nc.semaphore(name))

        ring = sb("ring", [128, CT, RING, PIXELS])
        blk = sb("blk", [128, 2 * DEEP, PIXELS])
        parts = sb("parts", [128, 2, 2, CT, PIXELS], FP16)
        geo_sb = sb("geo_sb", [128, G_END])
        had_sb = sb("had_sb", [128, CT, CT, 128], FP16)
        off_sb = sb("off_sb", [128, 2 * OFFSETS])
        px = sb("px", [128, 5, OFFSETS])
        wk = sb("wk", [128, 6, OFFSETS])
        rank = sb("rank", [128, OFFSETS])
        scrap = sb("scrap", [128, 4])
        count_f = sb("count_f", [128, 1])
        count_i = sb("count_i", [128, 1], INT32)
        sel = sb("sel", [128, FAST, 5])
        taps = sb("taps", [128, FAST, 44])
        norm = sb("norm", [128, FAST, 2])
        view = sb("view", [128, FAST, CHUNKS + 1])
        place_f = sb("place_f", [128, FAST, 4])
        place = sb("place", [128, FAST, 4], INT32)
        rows_f = sb("rows_f", [128, 2, ROW_LOTS, CT])
        rows = sb("rows", [128, 2, ROW_LOTS, CT], INT32)
        halfstat = sb("halfstat", [128, 4, CT - 1, 2, 6])
        pivot = sb("pivot", [128, BATCH])
        sums = sb("sums", [128, 2, BATCH])
        stat = sb("stat", [128, CT, BATCH, 2])
        gn = sb("gn", [128, BATCH, 2])
        tmp = sb("tmp", [128, 4, BATCH])
        moment = sb("moment", [128, CT, BATCH])
        blk_gn = sb("blk_gn", [128, DEEP, 2])
        blk_half = sb("blk_half", [128, DEEP, 2, 6])
        blk_stat = sb("blk_stat", [128, DEEP, 2])
        early = parts[:, :, :, :, :].rearrange("p a b c d -> p (a b c d)").bitcast(FP32)
        wide = early[:, 0:OFFSETS * OFFSETS]
        flip = early[:, 0:2 * PIXELS].rearrange("p (u j c) -> p u j c", u=2, c=128)
        conv_w = early[:, OFFSETS * OFFSETS:OFFSETS * OFFSETS + FAST * TAPS_Y * TAPS_X]\
            .rearrange("p (k y x) -> p k y x", k=FAST, y=TAPS_Y)

        ps = [ctx.enter_context(nc.psum_tensor(f"ps{n}", [128, 2, 512], FP32)) for n in range(4)]

        load_done = [sem(f"load_done{n}") for n in range(4)]
        const_in = sem("const_in")
        dve_link = sem("dve_link")
        stat_done = sem("stat_done")
        sum_stat_done = sem("sum_stat_done")
        rank_done = sem("rank_done")
        place_done = sem("place_done")
        exp_in = sem("exp_in")
        exp_done = sem("exp_done")
        conv_w_done = sem("conv_w_done")
        sum_in = sem("sum_in")
        sum_done = sem("sum_done")
        std_in = sem("std_in")
        std_done = sem("std_done")
        gn_done = sem("gn_done")
        x_in = [sem(f"x_in{u}") for u in range(DEEP)]
        shift_in = [sem(f"shift_in{u}") for u in range(DEEP)]
        gn_in = [sem(f"gn_in{u}") for u in range(DEEP)]
        centred = sem("centred")
        flipped = sem("flipped")
        flip_masked = sem("flip_masked")
        convolved = sem("convolved")
        x1_done = sem("x1_done")
        blk_stat_done = sem("blk_stat_done")
        blk_out = [sem(f"blk_out{u}") for u in range(DEEP)]
        xn_done = sem("xn_done")
        high_done = sem("high_done")
        low_done = sem("low_done")
        product_done = sem("product_done")
        result_done = sem("result_done")
        store_done = [sem(f"store_done{u}") for u in range(2)]
        reload_done = sem("reload_done")
        patch_done = [sem(f"patch_done{lot}") for lot in range(len(LOTS))]
        stat_patched = sem("stat_patched")
        gn_out = sem("gn_out")
        stat_out = sem("stat_out")
        more_link = sem("more_link")
        more_placed = sem("more_placed")
        more_exp_in = sem("more_exp_in")
        more_exp_done = sem("more_exp_done")
        more_conv_w = sem("more_conv_w")
        more_in = sem("more_in")
        more_centred = sem("more_centred")
        more_flipped = sem("more_flipped")
        more_masked = sem("more_masked")
        more_convolved = sem("more_convolved")
        more_ready = sem("more_ready")
        more_out = sem("more_out")
        more_patched = sem("more_patched")
        block = ctx.enter_context(nc.Block())

        def bc(ap, shape):
            return ap.broadcast_to(shape)

        @block.sync
        def _(sp):
            sp.dma_start(off_sb[:, :], bc(offset.rearrange("(a f) k -> a (f k)", a=1), [128, 2 * OFFSETS])).then_inc(const_in, 16)
            sp.dma_start(geo_sb[:, :], geo).then_inc(const_in, 16)
            sp.dma_start(had_sb[:, :, :, :], had.rearrange("p (t m n) -> p t m n", t=CT, m=CT)).then_inc(const_in, 16)
            for i in range(BATCH):
                if i >= 4:
                    sp.wait_ge(load_done[i % 4], 16 * (i // 4))
                if i >= RING:
                    sp.wait_ge(stat_done, i - RING + 1)
                    sp.wait_ge(sum_stat_done, i - RING + 1)
                sp.dma_start(ring[:, :, i % RING, :], x_bcp[i]).then_inc(load_done[i % 4], 16)

            def fetch_shifted(k):
                at = sp.value_load(place[0:1, k, 3:4], min_val=1, max_val=PIXELS * (CHANNELS - BIND + 2) - 1)
                if k >= DEEP:
                    sp.wait_ge(flipped, k - DEEP + 1)
                sp.dma_start(blk[:, DEEP + k % DEEP, :],
                             x_pad[:, ds(at, BIND * PIXELS)].rearrange("b (c n) -> b c n", c=BIND)).then_inc(shift_in[k % DEEP], 16)

            def fetch_plain(k):
                at = sp.value_load(place[0:1, k, 2:3], min_val=PIXELS, max_val=PIXELS * (CHANNELS - BIND + 1))
                if k >= DEEP:
                    sp.wait_ge(blk_out[k % DEEP], 32 * (k // DEEP))
                sp.dma_start(blk[:, k % DEEP, :],
                             x_pad[:, ds(at, BIND * PIXELS)].rearrange("b (c n) -> b c n", c=BIND)).then_inc(x_in[k % DEEP], 16)

            def fetch_gn(k):
                at = sp.value_load(place[0:1, k, 0:1], min_val=0, max_val=CHANNELS - BIND)
                if k >= DEEP:
                    sp.wait_ge(x1_done, k - DEEP + 1)
                sp.dma_start(blk_gn[:, k % DEEP, :], gn_rows[ds(at, BIND), :].rearrange("c (b k) -> b c k", k=2)).then_inc(gn_in[k % DEEP], 16)

            sp.wait_ge(place_done, 1)
            for k in range(DEEP):
                fetch_shifted(k)
                fetch_plain(k)
            sp.wait_ge(gn_done, 1)
            sp.dma_start(gn_rows.rearrange("(c t) n -> c t n", t=CT), bc(gn[:, :, :].rearrange("c (o b) k -> c o (b k)", o=1), [128, CT, 2 * BATCH])).then_inc(gn_out, 16)
            sp.wait_ge(gn_out, 16)
            for k in range(FAST + 1):
                if DEEP <= k < FAST:
                    fetch_shifted(k)
                if k < FAST:
                    fetch_gn(k)
                if k > DEEP:
                    fetch_plain(k - 1)

            active = sp.value_load(count_i[0:1, 0:1], min_val=0, max_val=OFFSETS)
            with sp.If(active > FAST):
                for u in range(DEEP):
                    sp.wait_ge(blk_out[u], 32 * blocks_in(u))
                with sp.Fori(FAST, OFFSETS) as k:
                    m = k - FAST
                    sp.wait_ge(more_placed, 1)
                    sp.sem_clear(more_placed)
                    c_at = sp.value_load(place[0:1, 0, 0:1], min_val=0, max_val=CHANNELS - BIND)
                    x_at = sp.value_load(place[0:1, 0, 2:3], min_val=PIXELS, max_val=PIXELS * (CHANNELS - BIND + 1))
                    s_at = sp.value_load(place[0:1, 0, 3:4], min_val=1, max_val=PIXELS * (CHANNELS - BIND + 2) - 1)
                    sp.dma_start(blk[:, 0, :], x_pad[:, ds(x_at, BIND * PIXELS)].rearrange("b (c n) -> b c n", c=BIND)).then_inc(more_in, 16)
                    sp.dma_start(blk[:, DEEP, :], x_pad[:, ds(s_at, BIND * PIXELS)].rearrange("b (c n) -> b c n", c=BIND)).then_inc(more_in, 16)
                    sp.dma_start(blk_gn[:, 0, :], gn_rows[ds(c_at, BIND), :].rearrange("c (b k) -> b c k", k=2)).then_inc(more_in, 16)
                    sp.wait_ge(more_ready, m + 1)
                    sp.dma_start(x1_more[ds(m * BIND, BIND), :].rearrange("c (b n) -> b c n", b=BATCH), blk[:, 0, :]).then_inc(more_out, 16)
                    sp.dma_start(stat_rows[ds(c_at, BIND), :].rearrange("c (b k) -> b c k", k=2), blk_stat[:, 0, :]).then_inc(more_out, 16)

            for u in range(DEEP):
                sp.wait_ge(blk_out[u], 32 * blocks_in(u))
            with sp.If(active > FAST):
                sp.wait_ge(more_out, 32 * (OFFSETS - FAST))
            sp.dma_start(stat[:, :, :, :].rearrange("p t b k -> p t (b k)"),
                         stat_rows.rearrange("(c t) n -> c t n", t=CT)).then_inc(stat_patched, 16)
            def store(i):
                n = i - EXTRA
                sp.wait_ge(result_done, CT * (n + 1))
                if n >= 2:
                    sp.wait_ge(store_done[n % 2], 16 * (n // 2))
                sp.dma_start(out_v[i % BATCH], ring[:, :, i % RING, :]).then_inc(store_done[n % 2], 16)

            for i in range(EXTRA, 2 * EXTRA + 2):
                store(i)
            for i in range(BATCH, BATCH + EXTRA):
                sp.dma_start(ring[:, :, i % RING, :], x_bcp[i - BATCH]).then_inc(reload_done, 16)
            for i in range(2 * EXTRA + 2, BATCH + EXTRA):
                store(i)
            for u in range(2):
                sp.wait_ge(store_done[u], 16 * (BATCH // 2))

        @block.gpsimd
        def _(pool):
            pool.wait_ge(rank_done, 1)
            for u in range(DEEP):
                pool.wait_ge(blk_out[u], 32 * blocks_in(u))
            active = pool.value_load(count_i[0:1, 0:1], min_val=0, max_val=OFFSETS)
            with pool.If(active > FAST):
                pool.wait_ge(more_out, 32 * (OFFSETS - FAST))

            def patch(table, which, lot, first, signal):
                for t in range(CT):
                    pool.indirect_dma_start(
                        ring[:, t, first % RING:first % RING + LOT, :].rearrange("p b n -> p (b n)"), None,
                        table.rearrange("c (q n) -> (c q) n", q=ROW_LOTS),
                        bass.IndirectOffsetOnAxis(ap=rows[:, which, (first % BATCH) // LOT, t:t + 1], axis=0),
                        bounds_check=table.shape[0] * ROW_LOTS - 1, oob_is_err=False).then_inc(signal, 16)

            for lot, (first, end) in enumerate(LOTS):
                if first == BATCH:
                    pool.wait_ge(reload_done, 16 * EXTRA)
                with pool.If(active > FAST):
                    patch(x1_more, 1, lot, first, more_patched)
                    pool.wait_ge(more_patched, 16 * CT * (lot + 1))
                patch(x1_rows, 0, lot, first, patch_done[lot])

        @block.scalar
        def _(act):
            act.wait_ge(exp_in, 1)
            act.activation(taps[:, :, :], taps[:, :, :], ACT.Exp, scale=-2.0).then_inc(exp_done, 1)
            for i in range(BATCH):
                act.wait_ge(load_done[i % 4], 16 * (i // 4 + 1))
                image = ring[:, CT - 1, i % RING, :]
                if i >= 2:
                    act.wait_ge(sum_stat_done, i - 1)
                unused = [ps[2 * (i % 2) + n][:, :, :].rearrange("p a n -> p (a n)") for n in range(2)]
                act.activation(pivot[:, i:i + 1], image[:, 0:1], ACT.Copy)
                act.activation(unused[0], image, ACT.Identity,
                               bias=image[:, 0:1], scale=-1.0, accum_out=sums[:, 0, i:i + 1])
                act.activation(unused[1], image, ACT.Square,
                               bias=image[:, 0:1], scale=-1.0, accum_out=sums[:, 1, i:i + 1]).then_inc(sum_stat_done, 1)
            act.wait_ge(std_in, 1)
            act.activation(tmp[:, 2, :], tmp[:, 2, :], ACT.Sqrt).then_inc(std_done, 1)

            def centre(k, u):
                act.wait_ge(shift_in[u], 16 * (k // DEEP + 1))
                act.wait_ge(gn_in[u], 16 * (k // DEEP + 1))
                act.activation(blk[:, DEEP + u, :], blk[:, DEEP + u, :], ACT.Identity,
                               bias=blk_gn[:, u, 0:1], scale=1.0).then_inc(centred, 1)

            def leave(k, u):
                c_at = act.value_load(place[0:1, k, 0:1], min_val=0, max_val=CHANNELS - BIND)
                act.wait_ge(x1_done, k + 1)
                act.dma_start(x1_rows[BIND * k:BIND * (k + 1), :].rearrange("c (b n) -> b c n", b=BATCH), blk[:, u, :]).then_inc(blk_out[u], 16)
                act.wait_ge(blk_stat_done, k + 1)
                act.dma_start(stat_rows[ds(c_at, BIND), :].rearrange("c (b k) -> b c k", k=2), blk_stat[:, u, :]).then_inc(blk_out[u], 16)

            act.wait_ge(gn_done, 1)
            act.dma_start(stat_rows.rearrange("(c t) n -> c t n", t=CT), stat[:, :, :, :].rearrange("c t b k -> c t (b k)")).then_inc(stat_out, 16)
            for k in range(FAST):
                centre(k, k % DEEP)
                if k == 1:
                    act.wait_ge(stat_out, 16)
                if k >= 2:
                    leave(k - 2, (k - 2) % DEEP)
            for k in range(FAST - 2, FAST):
                leave(k, k % DEEP)

            active = act.value_load(count_i[0:1, 0:1], min_val=0, max_val=OFFSETS)
            with act.If(active > FAST):
                with act.Fori(FAST, OFFSETS) as k:
                    m = k - FAST
                    act.wait_ge(more_exp_in, m + 1)
                    act.activation(taps[:, 0:1, :], taps[:, 0:1, :], ACT.Exp, scale=-2.0).then_inc(more_exp_done, 1)
                    act.wait_ge(more_in, 48 * m + 48)
                    act.activation(blk[:, DEEP, :], blk[:, DEEP, :], ACT.Identity,
                                   bias=blk_gn[:, 0, 0:1], scale=1.0).then_inc(more_centred, 1)

            act.wait_ge(std_in, 2)
            act.activation(tmp[:, 2, :], tmp[:, 2, :], ACT.Sqrt).then_inc(std_done, 1)
            act.wait_ge(gn_done, 2)

            def split(n, u, turn, i):
                for t in range(CT):
                    act.wait_ge(low_done, CT * (n - 1) + t + 1) if n >= 1 else None
                    act.activation(blk[:, t, :], ring[:, t, i % RING, :], ACT.Identity,
                                   bias=gn[:, i % BATCH, 1:2], scale=gn[:, i % BATCH, 0:1]).then_inc(xn_done, 1)
                if turn:
                    act.wait_ge(product_done, CT * (n - 1))
                for t in range(CT):
                    act.wait_ge(xn_done, CT * n + t + 1)
                    act.activation(parts[:, u, 0, t, :], blk[:, t, :], ACT.Copy).then_inc(high_done, 1)

            for i in range(EXTRA, BATCH + EXTRA):
                n = i - EXTRA
                for lot, (first, end) in enumerate(LOTS):
                    if i == first:
                        act.wait_ge(patch_done[lot], 16 * CT)
                split(n, n % 2, n // 2, i)

        @block.tensor
        def _(pe):
            pe.wait_ge(const_in, 48)

            def group_sums(turn):
                for step in range(2):
                    pe.wait_ge(sum_in, 2 * turn + step + 1)
                    for t in range(CT):
                        last = pe.matmul(ps[0][:, step, 0:BATCH], geo_sb[:, G_SUM:G_SUM + 128],
                                         stat[:, t, :, 0] if step == 0 else moment[:, t, :],
                                         start=(t == 0), stop=(t == CT - 1))
                    last.then_inc(sum_done, 1)

            group_sums(0)
            pe.wait_ge(gn_done, 1)
            pe.wait_ge(conv_w_done, 1)

            eye = geo_sb[:, G_EYE:G_EYE + 128]

            def transpose_block(pixels, shifted):
                for j in range(CHUNKS):
                    last = pe.transpose(pixels[:, j // 4, 128 * (j % 4):128 * (j % 4 + 1)],
                                        shifted[:, 128 * j:128 * (j + 1)], eye)
                return last

            def convolve_block(sums, pixels, weights):
                for bank in range(2):
                    seen = 16 * bank
                    for j in range(3 * bank, 3 * bank + 5):
                        lo = max(4 * j - 1, 16 * bank)
                        hi = min(4 * j + 5, 16 * bank + 16)
                        for a, b in ((lo, seen), (seen, hi)):
                            if a < b:
                                last = pe.matmul(sums[:, bank, 32 * (a - 16 * bank):32 * (b - 16 * bank)],
                                                 pixels[:, j, :], weights[:, a - (4 * j - 1):b - (4 * j - 1), :],
                                                 start=(j == 3 * bank), stop=(j == 3 * bank + 4 and b == hi))
                        seen = hi
                return last

            def transposes(k):
                pe.wait_ge(centred, k + 1)
                if k >= 2:
                    pe.wait_ge(flip_masked, k - 1)
                transpose_block(ps[k % 2], blk[:, DEEP + k % DEEP, :]).then_inc(flipped, 1)

            def convolve(k):
                pe.wait_ge(flip_masked, k + 1)
                if k >= 2:
                    pe.wait_ge(x1_done, k - 1)
                convolve_block(ps[2 + k % 2], flip[:, k % 2], conv_w[:, k]).then_inc(convolved, 1)

            transposes(0)
            for k in range(FAST):
                if k + 1 < FAST:
                    transposes(k + 1)
                convolve(k)

            pe.wait_ge(rank_done, 1)
            active = pe.value_load(count_i[0:1, 0:1], min_val=0, max_val=OFFSETS)
            with pe.If(active > FAST):
                pe.wait_ge(x1_done, FAST)
                with pe.Fori(FAST, OFFSETS) as k:
                    m = k - FAST
                    pe.wait_ge(more_centred, m + 1)
                    transpose_block(ps[0], blk[:, DEEP, :]).then_inc(more_flipped, 1)
                    pe.wait_ge(more_masked, m + 1)
                    pe.wait_ge(more_conv_w, m + 1)
                    convolve_block(ps[2], flip[:, 1], conv_w[:, 0]).then_inc(more_convolved, 1)

            group_sums(1)
            for n in range(BATCH):
                u = n % 2
                pe.wait_ge(low_done, CT * (n + 1))
                for m in range(CT):
                    if n >= 1:
                        pe.wait_ge(result_done, CT * (n - 1) + m + 1)
                    for h in range(2):
                        for t in range(CT):
                            for part in range(2):
                                last = pe.matmul(ps[m][:, h, :], had_sb[:, t, m, :],
                                                 parts[:, u, part, t, 512 * h:512 * (h + 1)],
                                                 start=(t == 0 and part == 0), stop=(t == CT - 1 and part == 1))
                    last.then_inc(product_done, 1)

        @block.vector
        def _(dve):
            links = [0]

            def link(ins):
                links[0] += 1
                ins.then_inc(dve_link, 1)
                dve.wait_ge(dve_link, links[0])

            dve.wait_ge(const_in, 48)
            iota = geo_sb[:, G_IOTA:G_IOTA + OFFSETS]
            off_v = off_sb[:, :].rearrange("p (f k) -> p k f", k=2)
            o, rnd = wk[:, 0:2, :], px[:, 1:3, :]
            link(dve.tensor_scalar(o, off_v, PX_SCALE, 64.0, ALU.mult, ALU.min))
            link(dve.tensor_scalar(o, o, -64.0, None, ALU.max))
            link(dve.tensor_scalar(wk[:, 2:4, :], o, ROUND, None, ALU.add))
            link(dve.tensor_scalar(rnd, wk[:, 2:4, :], ROUND, None, ALU.subtract))
            link(dve.tensor_tensor(px[:, 3:5, :], o, rnd, ALU.subtract))
            dve.tensor_copy(px[:, 0, :], iota)
            link(dve.tensor_tensor(wk[:, 4:6, :], rnd, rnd, ALU.mult))
            link(dve.tensor_scalar(wk[:, 4:6, :], wk[:, 4:6, :], FAR * FAR, None, ALU.is_lt))
            link(dve.tensor_tensor(wk[:, 0, :], wk[:, 4, :], wk[:, 5, :], ALU.mult))
            link(dve.tensor_reduce(count_f[:, :], wk[:, 0, :], AX.X, ALU.add))
            dve.tensor_copy(count_i[:, :], count_f[:, :])
            link(dve.scalar_tensor_tensor(wk[:, 1, :], wk[:, 0, :], -float(OFFSETS), iota, ALU.mult, ALU.add))
            wide_v = wide.rearrange("p (f g) -> p f g", f=OFFSETS)
            full = [128, OFFSETS, OFFSETS]
            link(dve.tensor_tensor(wide_v, bc(wk[:, 1:2, :], full),
                                   bc(wk[:, 1, :].rearrange("p (f o) -> p f o", o=1), full), ALU.is_lt))
            link(dve.tensor_reduce(rank[:, :], wide_v, AX.X, ALU.add))

            mine = wide[:, 0:CT * OFFSETS].rearrange("p (t f) -> p t f", t=CT)
            link(dve.tensor_tensor(mine, bc(rank[:, :].rearrange("p (o f) -> p o f", o=1), [128, CT, OFFSETS]),
                                   geo_sb[:, G_OWN:G_OWN + CT * OFFSETS].rearrange("p (t f) -> p t f", t=CT), ALU.mult))
            link(dve.tensor_reduce(rows_f[:, 0, 0, :], mine, AX.X, ALU.add))
            link(dve.scalar_tensor_tensor(rows_f[:, 0, 0, :], rows_f[:, 0, 0, :], float(BIND), geo_sb[:, G_SUB:G_SUB + CT], ALU.mult, ALU.add))
            for q in range(ROW_LOTS - 1, -1, -1):
                last = dve.tensor_scalar(rows_f[:, 0, q, :], rows_f[:, 0, 0, :], float(ROW_LOTS), float(q), ALU.mult, ALU.add)
            link(last)
            fast_rows = float(FAST * BIND * ROW_LOTS)
            link(dve.tensor_scalar(rows_f[:, 1, :, :], rows_f[:, 0, :, :], fast_rows - 0.5, 2.0 * CHANNELS * ROW_LOTS, ALU.is_lt, ALU.mult))
            link(dve.tensor_tensor(rows_f[:, 1, :, :], rows_f[:, 1, :, :], rows_f[:, 0, :, :], ALU.add))
            link(dve.tensor_scalar(rows_f[:, 1, :, :], rows_f[:, 1, :, :], fast_rows, None, ALU.subtract))
            dve.tensor_copy(rows[:, :, :, :], rows_f[:, :, :, :]).then_inc(rank_done, 1)

            def slot_parameters(slot_ids, n, link, placed, exp_in, exp_done, exp_count, weighed):
                keep = slice(0, n)
                shape = [128, n, OFFSETS]
                hit = wide[:, 0:n * OFFSETS].rearrange("p (k f) -> p k f", k=n)
                pick = wide[:, n * OFFSETS:2 * n * OFFSETS].rearrange("p (k f) -> p k f", k=n)
                rank_v = rank[:, :].rearrange("p (o f) -> p o f", o=1)
                link(dve.tensor_tensor(hit, bc(rank_v, shape), bc(slot_ids, shape), ALU.is_equal))
                for v in range(5):
                    link(dve.tensor_tensor(pick, hit, bc(px[:, v:v + 1, :], shape), ALU.mult))
                    link(dve.tensor_reduce(sel[:, keep, v], pick, AX.X, ALU.add))
                f, dx, dy = sel[:, keep, 0:1], sel[:, keep, 1:2], sel[:, keep, 2:3]
                link(dve.tensor_scalar(place_f[:, keep, 0:1], f, float(BIND), None, ALU.mult))
                link(dve.tensor_scalar(place_f[:, keep, 1:2], f, 0.0, None, ALU.mult))
                link(dve.tensor_scalar(place_f[:, keep, 2:3], f, float(BIND * PIXELS), float(PIXELS), ALU.mult, ALU.add))
                link(dve.scalar_tensor_tensor(place_f[:, keep, 3:4], dy, -float(WIDTH), dx, ALU.mult, ALU.subtract))
                link(dve.tensor_tensor(place_f[:, keep, 3:4], place_f[:, keep, 3:4], place_f[:, keep, 2:3], ALU.add))
                dve.tensor_copy(place[:, keep, :], place_f[:, keep, :]).then_inc(placed, 1)
                link(dve.tensor_tensor(taps[:, keep, 0:35], bc(geo_sb[:, G_DX:G_DX + 35].rearrange("p (o d) -> p o d", o=1), [128, n, 35]),
                                       bc(sel[:, keep, 3:4], [128, n, 35]), ALU.add))
                link(dve.tensor_tensor(taps[:, keep, 35:44], bc(geo_sb[:, G_DY:G_DY + 9].rearrange("p (o d) -> p o d", o=1), [128, n, 9]),
                                       bc(sel[:, keep, 4:5], [128, n, 9]), ALU.add))
                dve.tensor_tensor(taps[:, keep, :], taps[:, keep, :], taps[:, keep, :], ALU.mult).then_inc(exp_in, 1)
                link(dve.tensor_tensor(view[:, keep, 0:CHUNKS], bc(geo_sb[:, G_ROW:G_ROW + CHUNKS].rearrange("p (o d) -> p o d", o=1), [128, n, CHUNKS]),
                                       bc(dy, [128, n, CHUNKS]), ALU.subtract))
                link(dve.tensor_tensor(view[:, keep, CHUNKS:], bc(geo_sb[:, G_COL:G_COL + 1].rearrange("p (o d) -> p o d", o=1), [128, n, 1]),
                                       dx, ALU.subtract))
                link(dve.tensor_scalar(view[:, keep, :], view[:, keep, :], 15.5, None, ALU.subtract))
                link(dve.tensor_tensor(view[:, keep, :], view[:, keep, :], view[:, keep, :], ALU.mult))
                link(dve.tensor_scalar(view[:, keep, :], view[:, keep, :], 256.0, None, ALU.is_lt))
                link(dve.tensor_tensor(view[:, keep, 0:CHUNKS], view[:, keep, 0:CHUNKS], bc(view[:, keep, CHUNKS:], [128, n, CHUNKS]), ALU.mult))
                dve.wait_ge(exp_done, exp_count)
                link(dve.tensor_tensor(taps[:, keep, :], taps[:, keep, :],
                                       bc(geo_sb[:, G_NEAR:G_NEAR + 44].rearrange("p (o d) -> p o d", o=1), [128, n, 44]), ALU.mult))
                link(dve.tensor_reduce(norm[:, keep, 0:1], taps[:, keep, 32:35], AX.X, ALU.add))
                link(dve.tensor_reduce(norm[:, keep, 1:2], taps[:, keep, 41:44], AX.X, ALU.add))
                link(dve.reciprocal(norm[:, keep, :], norm[:, keep, :]))
                link(dve.tensor_tensor(taps[:, keep, 0:32], taps[:, keep, 0:32], bc(norm[:, keep, 0:1], [128, n, 32]), ALU.mult))
                link(dve.tensor_tensor(taps[:, keep, 35:41], taps[:, keep, 35:41], bc(norm[:, keep, 1:2], [128, n, 6]), ALU.mult))
                link(dve.tensor_tensor(conv_w[:, keep, :, :],
                                       bc(taps[:, keep, 35:41].rearrange("p k (y o) -> p k y o", o=1), [128, n, 6, 32]),
                                       bc(taps[:, keep, 0:32].rearrange("p k (o x) -> p k o x", o=1), [128, n, 6, 32]), ALU.mult))
                dve.tensor_copy(norm[:, keep, :], norm[:, keep, :]).then_inc(weighed, 1)

            def slot_ids(k, n):
                return geo_sb[:, ds(G_IOTA + k, n)].rearrange("p (k o) -> p k o", o=1)

            slot_parameters(slot_ids(0, FAST), FAST, link, place_done, exp_in, exp_done, 1, conv_w_done)

            def combine(i):
                dve.wait_ge(stat_done, i + 1)
                for t in range(CT - 1):
                    last = dve.bn_aggr(stat[:, t, i, :], halfstat[:, i % 4, t, :, :].rearrange("p h s -> p (h s)"))
                return last

            for i in range(BATCH):
                dve.wait_ge(load_done[i % 4], 16 * (i // 4 + 1))
                for t in range(CT - 1):
                    for h in range(2):
                        last = dve.bn_stats(halfstat[:, i % 4, t, h, :], ring[:, t, i % RING, 512 * h:512 * (h + 1)])
                last.then_inc(stat_done, 1)
                if i >= 1:
                    combine(i - 1)
            link(combine(BATCH - 1))
            dve.wait_ge(sum_stat_done, BATCH)
            deviation, second_moment = tmp[:, 2, :], tmp[:, 3, :]
            link(dve.tensor_scalar(deviation, sums[:, 0, :], 1.0 / PIXELS, None, ALU.mult))
            dve.tensor_tensor(stat[:, CT - 1, :, 0], pivot[:, :], deviation, ALU.subtract)
            link(dve.tensor_tensor(second_moment, deviation, deviation, ALU.mult))
            link(dve.scalar_tensor_tensor(stat[:, CT - 1, :, 1], sums[:, 1, :], 1.0 / PIXELS, second_moment, ALU.mult, ALU.subtract))

            def groupnorm(turn, second):
                mean = stat[:, :, :, 0]
                var = stat[:, :, :, 1]
                dve.memset(scrap[:, 0:1], 0.0).then_inc(sum_in, 1)
                dve.wait_ge(sum_done, 2 * turn + 1)
                group_mean = bc(tmp[:, 0:1, :], [128, CT, BATCH])
                link(dve.tensor_scalar(tmp[:, 0, :], ps[0][:, 0, 0:BATCH], 1.0 / GROUP, None, ALU.mult))
                link(dve.tensor_tensor(moment[:, :, :], mean, group_mean, ALU.subtract))
                link(dve.tensor_tensor(moment[:, :, :], moment[:, :, :], moment[:, :, :], ALU.mult))
                dve.tensor_tensor(moment[:, :, :], moment[:, :, :], var, ALU.add).then_inc(sum_in, 1)
                dve.wait_ge(sum_done, 2 * turn + 2)
                dve.tensor_scalar(tmp[:, 2, :], ps[0][:, 1, 0:BATCH], 1.0 / GROUP, EPS, ALU.mult, ALU.add).then_inc(std_in, 1)
                dve.wait_ge(std_done, turn + 1)
                link(dve.reciprocal(tmp[:, 3, :], tmp[:, 2, :]))
                if not second:
                    dve.tensor_scalar(gn[:, :, 0], tmp[:, 0, :], -1.0, None, ALU.mult)
                    link(dve.tensor_copy(gn[:, :, 1], tmp[:, 3, :]))
                else:
                    link(dve.tensor_scalar(gn[:, :, 0], tmp[:, 3, :], HALF_SCALE, None, ALU.mult))
                    link(dve.scalar_tensor_tensor(gn[:, :, 1], tmp[:, 0, :], -1.0, gn[:, :, 0], ALU.mult, ALU.mult))
                dve.memset(scrap[:, 1:2], 0.0).then_inc(gn_done, 1)

            groupnorm(0, False)

            def mask_pixels(pixels, shifted, k):
                return dve.tensor_tensor(pixels, shifted[:, :, :].rearrange("p a (j c) -> p (a j) c", c=128),
                                         bc(view[:, k, 0:CHUNKS].rearrange("p (j o) -> p j o", o=1), [128, CHUNKS, 128]), ALU.mult)

            def add_displaced(x1, sums, rstd):
                return dve.scalar_tensor_tensor(x1, sums[:, :, :].rearrange("p a n -> p (a n)"), rstd, x1, ALU.mult, ALU.add)

            def mask_block(k):
                dve.wait_ge(flipped, k + 1)
                if k >= 2:
                    dve.wait_ge(convolved, k - 1)
                mask_pixels(flip[:, k % 2], ps[k % 2], k).then_inc(flip_masked, 1)

            def add_block(k):
                u = k % DEEP
                dve.wait_ge(convolved, k + 1)
                dve.wait_ge(x_in[u], 16 * (k // DEEP + 1))
                add_displaced(blk[:, u, :], ps[2 + k % 2], blk_gn[:, u, 1:2]).then_inc(x1_done, 1)
                dve.wait_ge(x1_done, k + 1)
                for h in range(2):
                    last = dve.bn_stats(blk_half[:, u, h, :], blk[:, u, 512 * h:512 * (h + 1)])
                link(last)
                dve.bn_aggr(blk_stat[:, u, :], blk_half[:, u, :, :].rearrange("p h s -> p (h s)")).then_inc(blk_stat_done, 1)

            mask_block(0)
            for k in range(FAST):
                if k + 1 < FAST:
                    mask_block(k + 1)
                add_block(k)

            active = dve.value_load(count_i[0:1, 0:1], min_val=0, max_val=OFFSETS)
            with dve.If(active > FAST):
                dve.wait_ge(convolved, FAST)
                for u in range(DEEP):
                    dve.wait_ge(blk_out[u], 32 * blocks_in(u))
                with dve.Fori(FAST, OFFSETS) as k:
                    m = k - FAST
                    step = [0]

                    def more(ins):
                        step[0] += 1
                        ins.then_inc(more_link, 1)
                        dve.wait_ge(more_link, MORE_LINKS * m + step[0])

                    slot_parameters(slot_ids(k, 1), 1, more, more_placed, more_exp_in, more_exp_done, m + 1, more_conv_w)
                    dve.wait_ge(more_flipped, m + 1)
                    mask_pixels(flip[:, 1], ps[0], 0).then_inc(more_masked, 1)
                    dve.wait_ge(more_convolved, m + 1)
                    more(add_displaced(blk[:, 0, :], ps[2], blk_gn[:, 0, 1:2]))
                    for h in range(2):
                        last = dve.bn_stats(blk_half[:, 0, h, :], blk[:, 0, 512 * h:512 * (h + 1)])
                    more(last)
                    dve.memset(scrap[:, 2:3], 0.0)
                    dve.bn_aggr(blk_stat[:, 0, :], blk_half[:, 0, :, :].rearrange("p h s -> p (h s)")).then_inc(more_ready, 1)
                    dve.wait_ge(more_out, 32 * m + 32)
                    dve.memset(scrap[:, 3:4], 0.0)
                    assert step[0] == MORE_LINKS, step[0]

            dve.wait_ge(stat_patched, 16)
            groupnorm(1, True)

            def result(n, m):
                i = n + EXTRA
                dve.wait_ge(product_done, CT * n + m + 1)
                dve.scalar_tensor_tensor(ring[:, m, i % RING, :], ps[m][:, :, :].rearrange("p a n -> p (a n)"),
                                         1.0 / (HALF_SCALE * float(np.sqrt(TARGET))), ring[:, m, i % RING, :],
                                         ALU.mult, ALU.add).then_inc(result_done, 1)

            for n in range(BATCH):
                u = n % 2
                for t in range(CT):
                    dve.wait_ge(high_done, CT * n + t + 1)
                    if n >= 2:
                        dve.wait_ge(product_done, CT * (n - 1))
                    dve.tensor_tensor(parts[:, u, 1, t, :], blk[:, t, :], parts[:, u, 0, t, :], ALU.subtract).then_inc(low_done, 1)
                    if n >= 1:
                        result(n - 1, t)
            for m in range(CT):
                result(BATCH - 1, m)


def kernel(x, L0_conv_offset):
    import concourse.bacc as bacc
    from concourse.bass_utils import run_bass_kernel_spmd

    x = np.ascontiguousarray(x)
    x_pad = np.zeros((BATCH, (CHANNELS + 2) * PIXELS), x.dtype)
    x_pad[:, PIXELS:PIXELS * (CHANNELS + 1)] = x.reshape(BATCH, -1)
    arrays = {"x_pad": x_pad, "offset": np.ascontiguousarray(L0_conv_offset),
              "geo": geometry_constants(), "had": hadamard_constants()}
    nc = bacc.Bacc("TRN2", target_bir_lowering=False, num_devices=1)
    args = [nc.dram_tensor(name, a.shape, mybir.dt.from_np(a.dtype), kind="ExternalInput").ap() for name, a in arrays.items()]
    out = nc.dram_tensor("out", (BATCH, CHANNELS, HEIGHT, WIDTH), FP32, kind="ExternalOutput").ap()
    build(nc, *args, out)
    r = run_bass_kernel_spmd(nc, [arrays], core_ids=[0])
    return r.results[0]["out"]
```

```python
import numpy as np
import concourse.bass as bass
from concourse import mybir
from contextlib import ExitStack

FP32 = mybir.dt.float32
FP16 = mybir.dt.float16
INT32 = mybir.dt.int32
ALU = mybir.AluOpType
ACT = mybir.ActivationFunctionType
AX = mybir.AxisListType

BATCH, CHANNELS, HEIGHT, WIDTH = 16, 384, 32, 32
PIXELS = HEIGHT * WIDTH
OFFSETS = 48
BIND = CHANNELS // OFFSETS
PX_SCALE = 64.0
CT = CHANNELS // 128
GROUP = CHANNELS // 32
EPS = 1e-5
TARGET = 512
ROUND = 12582912.0
FAR = 31.5
HALF_SCALE = 256.0

RING = 12
EXTRA = BATCH - RING
DEEP = 3
EARLY = 2
FAST = 9
TAPS_X, TAPS_Y = WIDTH, 6
MORE_LINKS = 33
CHUNKS = 8
LATE_PATCH = {4: (0, 1), 5: (2,), 6: (3,), 7: (4, 5)}

SUM_PAIRS = [(a, b) for a in range(CT) for b in range(CT) if abs(a - b) <= 1]

CLUSTER = 8
CLUSTERS = OFFSETS // CLUSTER
SP_CLUSTERS, ACT_CLUSTERS = (0, 5, 2), (4, 1, 3)

POOL_LOW = range(3, BATCH, 2)

BY_TILE = (0, BATCH - 2, BATCH - 1)

G_IOTA, G_DX, G_DY, G_NEAR = 0, 48, 83, 92
G_ROW = G_NEAR + 44
G_COL = G_ROW + CHUNKS
G_SPAN = G_COL + 1
G_INSIDE = G_SPAN + WIDTH + 2
G_EYE = G_INSIDE + WIDTH + 2
G_SUM = G_EYE + 128
G_END = G_SUM + 128 * len(SUM_PAIRS)


def geometry_constants():
    g = np.zeros((128, G_END), np.float32)
    p = np.arange(128)
    yi, xi = p // WIDTH, p % WIDTH
    g[:, G_IOTA:G_IOTA + OFFSETS] = np.arange(OFFSETS)
    g[:, G_DX:G_DX + 32] = xi[:, None] - np.arange(32)[None]
    g[:, G_DX + 32:G_DX + 35] = [-1, 0, 1]
    g[:, G_DY:G_DY + 6] = yi[:, None] - np.arange(6)[None] + 1
    g[:, G_DY + 6:G_DY + 9] = [-1, 0, 1]
    g[:, G_NEAR:G_NEAR + 44] = np.abs(g[:, G_DX:G_DX + 44]) <= 1
    g[:, G_ROW:G_ROW + CHUNKS] = 4 * np.arange(CHUNKS)[None] + yi[:, None]
    g[:, G_COL] = xi
    g[:, G_SPAN:G_INSIDE] = np.arange(-1, WIDTH + 1)
    g[:, G_INSIDE + 1:G_INSIDE + 1 + WIDTH] = 1
    g[:, G_EYE:G_EYE + 128] = np.eye(128)
    for n, (a, b) in enumerate(SUM_PAIRS):
        g[:, G_SUM + 128 * n:G_SUM + 128 * (n + 1)] = (128 * b + p[:, None]) // GROUP == (128 * a + p[None]) // GROUP
    return g


def hadamard_constants():
    h = np.array([[1.0]], np.float32)
    while h.shape[0] < 128:
        h = np.block([[h, h], [h, -h]])
    return np.concatenate([h, -h], axis=1).astype(np.float16)


def place_of(i):
    return (i - EXTRA) % RING


def blocks_in(u):
    return (FAST - u + DEEP - 1) // DEEP


def build(nc, x_pad, offset, geo, had, out):
    ds = bass.ds
    x1_rows = nc.dram_tensor("x1_rows", [CHANNELS, BATCH * PIXELS], FP32).ap()
    stat_rows = nc.dram_tensor("stat_rows", [CHANNELS, BATCH * 2], FP32).ap()
    gn_rows = nc.dram_tensor("gn_rows", [CHANNELS, BATCH * 2], FP32).ap()
    x_bcp = x_pad[:, PIXELS:PIXELS + CHANNELS * PIXELS].rearrange("b (t c n) -> b c t n", t=CT, c=128)
    out_v = out.rearrange("b (t c) h w -> b c t (h w)", t=CT)
    ctx = ExitStack()
    with ctx:
        def sb(name, shape, dt=FP32):
            return ctx.enter_context(nc.sbuf_tensor(name, shape, dt))

        def sem(name):
            return ctx.enter_context(nc.semaphore(name))

        ring = sb("ring", [128, CT, RING, PIXELS])
        blk = sb("blk", [128, 2 * DEEP, PIXELS])
        other_a = sb("other_a", [128, PIXELS])
        parts = sb("parts", [128, 2, 2, CT, PIXELS], FP16)
        geo_sb = sb("geo_sb", [128, G_END])
        had_sb = sb("had_sb", [128, 2, 128], FP16)
        off_sb = sb("off_sb", [128, 2 * OFFSETS])
        rank = sb("rank", [128, OFFSETS])
        scrap = sb("scrap", [128, 4])
        count_f = sb("count_f", [128, 1])
        count_i = sb("count_i", [128, 1], INT32)
        sel = sb("sel", [128, FAST, 5])
        norm = sb("norm", [128, FAST, 2])
        view = sb("view", [128, FAST, CHUNKS + 1])
        place = sb("place", [128, FAST, 3], INT32)
        rows = sb("rows", [128, OFFSETS + CLUSTERS], INT32)
        halfstat = sb("halfstat", [128, 4, CT - 1, 2, 6])
        pivot = sb("pivot", [128, BATCH])
        sums = sb("sums", [128, 2, BATCH])
        stat = sb("stat", [128, CT, BATCH, 2])
        gn = sb("gn", [128, CT, BATCH, 2])
        tmp = sb("tmp", [128, 3, CT, BATCH])
        moment = sb("moment", [128, CT, 2, BATCH])
        blk_gn = sb("blk_gn", [128, FAST, 2])
        blk_half = sb("blk_half", [128, DEEP, 2, 6])
        blk_stat = sb("blk_stat", [128, DEEP, 2])
        early = parts[:, :, :, :, :].rearrange("p a b c d -> p (a b c d)").bitcast(FP32)
        wide = early[:, 0:OFFSETS * OFFSETS]
        flip = early[:, 0:2 * PIXELS].rearrange("p (u j c) -> p u j c", u=2, c=128)
        conv_w = early[:, OFFSETS * OFFSETS:OFFSETS * OFFSETS + FAST * TAPS_Y * TAPS_X]\
            .rearrange("p (k y x) -> p k y x", k=FAST, y=TAPS_Y)
        spare = OFFSETS * OFFSETS + FAST * TAPS_Y * TAPS_X
        px = early[:, spare:spare + 5 * OFFSETS].rearrange("p (v f) -> p v f", v=5)
        spare += 5 * OFFSETS
        wk = early[:, spare:spare + 6 * OFFSETS].rearrange("p (v f) -> p v f", v=6)
        spare += 6 * OFFSETS
        taps = early[:, spare:spare + FAST * 44].rearrange("p (k d) -> p k d", k=FAST)
        spare += FAST * 44
        place_f = early[:, spare:spare + FAST * 3].rearrange("p (k d) -> p k d", k=FAST)
        axes = EARLY * 2
        in_view = wk.rearrange("p v f -> p (v f)")[:, 0:axes * (WIDTH + 2)].rearrange("p (k a c) -> p k a c", k=EARLY, a=2)
        product = wk.rearrange("p v f -> p (v f)")[:, axes * (WIDTH + 2):axes * (2 * WIDTH + 2)]\
            .rearrange("p (k a c) -> p k a c", k=EARLY, a=2)
        tap3 = wk.rearrange("p v f -> p (v f)")[:, axes * (2 * WIDTH + 2):axes * (2 * WIDTH + 5)]\
            .rearrange("p (k a c) -> p k a c", k=EARLY, a=2)
        share = early[:, 2 * PIXELS:2 * PIXELS + axes * WIDTH].rearrange("p (k a c) -> p k a c", k=EARLY, a=2)
        aside = [other_a[:, :], early[:, 5 * PIXELS:6 * PIXELS]]

        ps = [ctx.enter_context(nc.psum_tensor(f"ps{n}", [128, 2, 512], FP32)) for n in range(4)]

        load_done = [sem(f"load_done{n}") for n in range(4)]
        const_in = sem("const_in")
        dve_link = sem("dve_link")
        stat_done = sem("stat_done")
        sum_stat_done = sem("sum_stat_done")
        rank_done = sem("rank_done")
        place_done = sem("place_done")
        exp_in = sem("exp_in")
        exp_done = sem("exp_done")
        conv_w_done = sem("conv_w_done")
        sum_in = sem("sum_in")
        sum_done = sem("sum_done")
        std_in = sem("std_in")
        std_done = sem("std_done")
        gn_done = sem("gn_done")
        x_in = [sem(f"x_in{u}") for u in range(DEEP)]
        shift_in = [sem(f"shift_in{u}") for u in range(DEEP)]
        gn_in = [sem(f"gn_in{k}") for k in range(FAST)]
        centred = sem("centred")
        slope_ready = sem("slope_ready")
        mean_share = sem("mean_share")
        partial_done = sem("partial_done")
        flipped = sem("flipped")
        flip_masked = sem("flip_masked")
        convolved = sem("convolved")
        x1_done = sem("x1_done")
        blk_stat_done = sem("blk_stat_done")
        blk_out = [sem(f"blk_out{u}") for u in range(DEEP)]
        xn_done = [sem(f"xn_done{t}") for t in range(CT)]
        mixed = [sem(f"mixed_{name}") for name in ("a", "b")]
        high_done = [sem(f"high_done_{name}") for name in ("a", "b", "w")]
        low_done = [sem(f"low_done_{name}") for name in ("a", "b", "w")]
        product_done = sem("product_done")
        result_done = sem("result_done")
        store_done = [sem(f"store_done{u}") for u in range(2)]
        reload_done = sem("reload_done")
        patch_done = sem("patch_done")
        late_patch_done = sem("late_patch_done")
        stat_patched = sem("stat_patched")
        gn_out = sem("gn_out")
        stat_out = sem("stat_out")
        more_link = sem("more_link")
        more_placed = sem("more_placed")
        more_exp_in = sem("more_exp_in")
        more_exp_done = sem("more_exp_done")
        more_conv_w = sem("more_conv_w")
        more_in = sem("more_in")
        more_centred = sem("more_centred")
        more_flipped = sem("more_flipped")
        more_masked = sem("more_masked")
        more_convolved = sem("more_convolved")
        more_ready = sem("more_ready")
        more_out = sem("more_out")
        more_patched = sem("more_patched")
        block = ctx.enter_context(nc.Block())

        def bc(ap, shape):
            return ap.broadcast_to(shape)

        def first_tile(n):
            return blk[:, n % 2, :]

        def last_tile(n):
            return blk[:, 2 + n % 2, :]

        middle = blk[:, 4, :]

        def sum_a(n):
            return blk[:, 5, :] if n % 2 == 0 else other_a[:, :]

        def mix_a(eng, n):
            eng.wait_ge(xn_done[0], n + 1)
            eng.wait_ge(xn_done[2], n + 1)
            if n >= 2:
                eng.wait_ge(low_done[0], n - 1)
            eng.tensor_tensor(sum_a(n), first_tile(n), last_tile(n), ALU.add).then_inc(mixed[0], 1)

        def mix_b(eng, n):
            eng.wait_ge(mixed[0], n + 1)
            eng.tensor_tensor(last_tile(n), first_tile(n), last_tile(n), ALU.subtract).then_inc(mixed[1], 1)

        def low(eng, n, s, source):
            eng.wait_ge(high_done[s], n + 1)
            if n >= 2:
                eng.wait_ge(product_done, CT * (n - 1))
            eng.tensor_tensor(parts[:, n % 2, 1, s, :], source, parts[:, n % 2, 0, s, :], ALU.subtract).then_inc(low_done[s], 1)

        def patch(eng, clusters, first, count, signal, ready=None):
            def row_of(n):
                return eng.value_load(rows[0:1, n:n + 1], min_val=0, max_val=CHANNELS - BIND)

            def fetch(f, row):
                tile, part = BIND * f // 128, BIND * f % 128
                eng.dma_start(ring[part:part + BIND, tile, 0:count, :],
                              x1_rows[ds(row, BIND), first * PIXELS:(first + count) * PIXELS]
                              .rearrange("c (b n) -> c b n", n=PIXELS)).then_inc(signal, 16)

            at = {}
            if ready is not None and first:
                at = {n: row_of(n) for cluster in clusters
                      for n in (OFFSETS + cluster, *range(CLUSTER * cluster, CLUSTER * (cluster + 1)))}
            for cluster in clusters:
                members = range(CLUSTER * cluster, CLUSTER * (cluster + 1))
                if ready is None:
                    for f in members:
                        fetch(f, row_of(f))
                else:
                    with eng.If((at[OFFSETS + cluster] if at else row_of(OFFSETS + cluster)) < FAST * BIND):
                        rows_of = [at[f] if at else row_of(f) for f in members]
                        for f, row in zip(members, rows_of):
                            with eng.If(row < FAST * BIND):
                                ready()
                                fetch(f, row)

        def fast_blocks_out(eng):
            for u in range(DEEP):
                eng.wait_ge(blk_out[u], 32 * blocks_in(u))

        def patch_kept(eng, clusters, active):
            with eng.If(active > FAST):
                eng.wait_ge(more_out, 32 * (OFFSETS - FAST))
                fast_blocks_out(eng)
                patch(eng, clusters, EXTRA, RING, more_patched)
                eng.wait_ge(more_patched, 16 * OFFSETS)
            patch(eng, clusters, EXTRA, RING, patch_done, lambda: fast_blocks_out(eng))

        def fetch_gn(eng, k):
            at = eng.value_load(place[0:1, k, 0:1], min_val=0, max_val=CHANNELS - BIND)
            eng.dma_start(blk_gn[:, k, :], gn_rows[ds(at, BIND), :].rearrange("c (b k) -> b c k", k=2)).then_inc(gn_in[k], 16)

        @block.sync
        def _(sp):
            sp.dma_start(off_sb[:, :], bc(offset.rearrange("(a f) k -> a (f k)", a=1), [128, 2 * OFFSETS])).then_inc(const_in, 16)
            sp.dma_start(geo_sb[:, :], geo).then_inc(const_in, 16)
            sp.dma_start(had_sb[:, :, :], had.rearrange("p (s n) -> p s n", s=2)).then_inc(const_in, 16)
            def fetch_shifted(k):
                at = sp.value_load(place[0:1, k, 2:3], min_val=1, max_val=PIXELS * (CHANNELS - BIND + 2) - 1)
                if k >= DEEP:
                    sp.wait_ge(flipped, k - DEEP + 1)
                sp.dma_start(blk[:, DEEP + k % DEEP, :],
                             x_pad[:, ds(at, BIND * PIXELS)].rearrange("b (c n) -> b c n", c=BIND)).then_inc(shift_in[k % DEEP], 16)

            def fetch_plain(k):
                at = sp.value_load(place[0:1, k, 1:2], min_val=PIXELS, max_val=PIXELS * (CHANNELS - BIND + 1))
                if k >= DEEP:
                    sp.wait_ge(blk_out[k % DEEP], 32 * (k // DEEP))
                sp.dma_start(blk[:, k % DEEP, :],
                             x_pad[:, ds(at, BIND * PIXELS)].rearrange("b (c n) -> b c n", c=BIND)).then_inc(x_in[k % DEEP], 16)

            for i in range(BATCH):
                if i >= 4:
                    sp.wait_ge(load_done[i % 4], 16 * (i // 4))
                if i >= RING:
                    sp.wait_ge(stat_done, i - RING + 1)
                    sp.wait_ge(sum_stat_done, i - RING + 1)
                sp.dma_start(ring[:, :, place_of(i), :], x_bcp[i]).then_inc(load_done[i % 4], 16)
                if i == RING - 1:
                    sp.wait_ge(place_done, 1)
                    for k in range(EARLY):
                        fetch_shifted(k)

            for k in range(EARLY, DEEP + EARLY):
                fetch_shifted(k)
            for k in range(DEEP):
                fetch_plain(k)
            sp.wait_ge(gn_done, 1)
            sp.dma_start(gn_rows.rearrange("(t c) n -> c t n", t=CT), gn[:, :, :, :].rearrange("c t b k -> c t (b k)")).then_inc(gn_out, 16)
            sp.wait_ge(gn_out, 16)
            for k in range(EARLY):
                fetch_gn(sp, k)
            for k in range(DEEP + EARLY, FAST + 2):
                if k < FAST:
                    fetch_gn(sp, k)
                    fetch_shifted(k)
                fetch_plain(k - 2)

            active = sp.value_load(count_i[0:1, 0:1], min_val=0, max_val=OFFSETS)
            with sp.If(active > FAST):
                for u in range(DEEP):
                    sp.wait_ge(blk_out[u], 32 * blocks_in(u))
                with sp.Fori(FAST, OFFSETS) as k:
                    m = k - FAST
                    sp.wait_ge(more_placed, 1)
                    sp.sem_clear(more_placed)
                    c_at = sp.value_load(place[0:1, 0, 0:1], min_val=0, max_val=CHANNELS - BIND)
                    x_at = sp.value_load(place[0:1, 0, 1:2], min_val=PIXELS, max_val=PIXELS * (CHANNELS - BIND + 1))
                    s_at = sp.value_load(place[0:1, 0, 2:3], min_val=1, max_val=PIXELS * (CHANNELS - BIND + 2) - 1)
                    sp.dma_start(blk[:, 0, :], x_pad[:, ds(x_at, BIND * PIXELS)].rearrange("b (c n) -> b c n", c=BIND)).then_inc(more_in, 16)
                    sp.dma_start(blk[:, DEEP, :], x_pad[:, ds(s_at, BIND * PIXELS)].rearrange("b (c n) -> b c n", c=BIND)).then_inc(more_in, 16)
                    sp.dma_start(blk_gn[:, 0, :], gn_rows[ds(c_at, BIND), :].rearrange("c (b k) -> b c k", k=2)).then_inc(more_in, 16)
                    sp.wait_ge(more_ready, m + 1)
                    sp.dma_start(x1_rows[ds(k * BIND, BIND), :].rearrange("c (b n) -> b c n", b=BATCH), blk[:, 0, :]).then_inc(more_out, 16)
                    sp.dma_start(stat_rows[ds(c_at, BIND), :].rearrange("c (b k) -> b c k", k=2), blk_stat[:, 0, :]).then_inc(more_out, 16)

            def stored(n):
                return 16 * sum(CT if i in BY_TILE else 1 for i in range(n % 2, n + 1, 2))

            def store(n):
                i = n + EXTRA
                if n >= 2:
                    sp.wait_ge(store_done[n % 2], stored(n - 2))
                if n in BY_TILE:
                    for t in range(CT):
                        sp.wait_ge(result_done, CT * n + t + 1)
                        sp.dma_start(out_v[i % BATCH][:, t, :], ring[:, t, place_of(i), :]).then_inc(store_done[n % 2], 16)
                else:
                    sp.wait_ge(result_done, CT * (n + 1))
                    sp.dma_start(out_v[i % BATCH], ring[:, :, place_of(i), :]).then_inc(store_done[n % 2], 16)

            def reload(j):
                sp.wait_ge(store_done[j % 2], stored(j))
                sp.dma_start(ring[:, :, j, :], x_bcp[j]).then_inc(reload_done, 16)

            patch_kept(sp, SP_CLUSTERS, active)
            for n in range(BATCH):
                if n in (1, EXTRA):
                    reload(n - 1)
                store(n)
                if 1 < n < EXTRA:
                    reload(n - 1)
                if n in LATE_PATCH:
                    if n == min(LATE_PATCH):
                        with sp.If(active > FAST):
                            sp.wait_ge(reload_done, 16 * EXTRA)
                            patch(sp, range(CLUSTERS), 0, EXTRA, more_patched)
                            sp.wait_ge(more_patched, 16 * 2 * OFFSETS)
                    patch(sp, LATE_PATCH[n], 0, EXTRA, late_patch_done, lambda: sp.wait_ge(reload_done, 16 * EXTRA))
            for n in range(BATCH - 2, BATCH):
                sp.wait_ge(store_done[n % 2], stored(n))

        @block.gpsimd
        def _(pool):
            def leave(k, u):
                c_at = pool.value_load(place[0:1, k, 0:1], min_val=0, max_val=CHANNELS - BIND)
                pool.wait_ge(x1_done, k + 1)
                pool.dma_start(x1_rows[BIND * k:BIND * (k + 1), :].rearrange("c (b n) -> b c n", b=BATCH), blk[:, u, :]).then_inc(blk_out[u], 16)
                pool.wait_ge(blk_stat_done, k + 1)
                pool.dma_start(stat_rows[ds(c_at, BIND), :].rearrange("c (b k) -> b c k", k=2), blk_stat[:, u, :]).then_inc(blk_out[u], 16)

            image = [128, HEIGHT, WIDTH]
            for k in range(EARLY):
                pool.wait_ge(slope_ready, k + 1)
                pool.tensor_tensor(aside[k].rearrange("p (y x) -> p y x", y=HEIGHT),
                                   bc(share[:, k, 1, :].rearrange("p (y o) -> p y o", o=1), image),
                                   bc(share[:, k, 0, :].rearrange("p (o x) -> p o x", o=1), image), ALU.mult).then_inc(mean_share, 1)
            pool.wait_ge(rank_done, 1)
            pool.wait_ge(place_done, 1)
            pool.wait_ge(stat_out, 16)
            for k in range(FAST):
                leave(k, k % DEEP)
            active = pool.value_load(count_i[0:1, 0:1], min_val=0, max_val=OFFSETS)
            fast_blocks_out(pool)
            with pool.If(active > FAST):
                pool.wait_ge(more_out, 32 * (OFFSETS - FAST))
            pool.dma_start(stat[:, :, :, :].rearrange("p t b k -> p t (b k)"),
                          stat_rows.rearrange("(t c) n -> c t n", t=CT)).then_inc(stat_patched, 16)

            for s in range(2):
                pool.wait_ge(high_done[s], 1)
            for n in range(1, BATCH):
                mix_a(pool, n)
                mix_b(pool, n)
                if n in POOL_LOW:
                    low(pool, n, 2, middle)

        @block.scalar
        def _(act):
            act.wait_ge(exp_in, 1)
            act.activation(taps[:, :, :], taps[:, :, :], ACT.Exp, scale=-2.0).then_inc(exp_done, 1)
            for i in range(BATCH):
                act.wait_ge(load_done[i % 4], 16 * (i // 4 + 1))
                image = ring[:, CT - 1, place_of(i), :]
                if i >= 1:
                    act.wait_ge(sum_stat_done, i)
                act.activation(pivot[:, i:i + 1], image[:, 0:1], ACT.Copy)
                act.activation(aside[0], image, ACT.Identity,
                               bias=image[:, 0:1], scale=-1.0, accum_out=sums[:, 0, i:i + 1])
                act.activation(aside[1], image, ACT.Square,
                               bias=image[:, 0:1], scale=-1.0, accum_out=sums[:, 1, i:i + 1]).then_inc(sum_stat_done, 1)
                k = i - RING
                if 0 <= k < EARLY:
                    act.wait_ge(conv_w_done, 1)
                    act.wait_ge(flipped, k + 1)
                    for j in range(CHUNKS):
                        last = act.activation(flip[:, k, j, :], ps[k][:, j // 4, 128 * (j % 4):128 * (j % 4 + 1)],
                                              ACT.Copy, scale=view[:, k, j:j + 1])
                    last.then_inc(flip_masked, 1)
            act.wait_ge(std_in, 1)
            act.activation(tmp[:, 1, :, :], tmp[:, 1, :, :], ACT.Sqrt).then_inc(std_done, 1)

            def centre(k, u):
                act.wait_ge(shift_in[u], 16 * (k // DEEP + 1))
                act.wait_ge(gn_in[k], 16)
                act.activation(blk[:, DEEP + u, :], blk[:, DEEP + u, :], ACT.Identity,
                               bias=blk_gn[:, k, 0:1], scale=1.0).then_inc(centred, 1)

            act.wait_ge(gn_done, 1)
            act.dma_start(stat_rows.rearrange("(t c) n -> c t n", t=CT), stat[:, :, :, :].rearrange("c t b k -> c t (b k)")).then_inc(stat_out, 16)
            act.wait_ge(gn_out, 16)
            for k in range(EARLY, DEEP + EARLY):
                fetch_gn(act, k)
            for k in range(EARLY, FAST):
                centre(k, k % DEEP)

            active = act.value_load(count_i[0:1, 0:1], min_val=0, max_val=OFFSETS)
            with act.If(active > FAST):
                with act.Fori(FAST, OFFSETS) as k:
                    m = k - FAST
                    act.wait_ge(more_exp_in, m + 1)
                    act.activation(taps[:, 0:1, :], taps[:, 0:1, :], ACT.Exp, scale=-2.0).then_inc(more_exp_done, 1)
                    act.wait_ge(more_in, 48 * m + 48)
                    act.activation(blk[:, DEEP, :], blk[:, DEEP, :], ACT.Identity,
                                   bias=blk_gn[:, 0, 0:1], scale=1.0).then_inc(more_centred, 1)

            patch_kept(act, ACT_CLUSTERS, active)
            act.wait_ge(std_in, 2)
            act.activation(tmp[:, 1, :, :], tmp[:, 1, :, :], ACT.Sqrt).then_inc(std_done, 1)
            act.wait_ge(gn_done, 2)

            def normalise(n, t, target):
                i = n + EXTRA
                act.activation(target, ring[:, t, place_of(i), :], ACT.Identity,
                               bias=gn[:, t, i % BATCH, 1:2], scale=gn[:, t, i % BATCH, 0:1]).then_inc(xn_done[t], 1)

            def outer_tiles(n):
                if n == RING:
                    act.wait_ge(late_patch_done, 16 * FAST)
                if n >= 2:
                    act.wait_ge(mixed[1], n - 1)
                normalise(n, 0, first_tile(n))
                if n >= 2:
                    act.wait_ge(low_done[1], n - 1)
                normalise(n, 2, last_tile(n))

            def middle_tile(n):
                if n >= 1:
                    act.wait_ge(low_done[2], n)
                normalise(n, 1, middle)
                if n >= 2:
                    act.wait_ge(product_done, CT * (n - 1))
                act.wait_ge(xn_done[1], n + 1)
                high(n, 2, middle)

            def high_a(n):
                act.wait_ge(mixed[0], n + 1)
                high(n, 0, sum_a(n))

            def high_b(n):
                act.wait_ge(mixed[1], n + 1)
                high(n, 1, last_tile(n))

            def high(n, s, source):
                act.activation(parts[:, n % 2, 0, s, :], source, ACT.Copy).then_inc(high_done[s], 1)

            act.wait_ge(patch_done, 16 * FAST)
            outer_tiles(0)
            middle_tile(0)
            for n in range(BATCH):
                if n == 0:
                    high_a(n)
                if n + 1 < BATCH:
                    outer_tiles(n + 1)
                if n > 0:
                    high_a(n)
                high_b(n)
                if n + 1 < BATCH:
                    middle_tile(n + 1)

        @block.tensor
        def _(pe):
            pe.wait_ge(const_in, 48)

            def group_sums(count, bank, values):
                pe.wait_ge(sum_in, count)
                for n, (a, b) in enumerate(SUM_PAIRS):
                    rhs = values(b)
                    width = rhs.shape[-1]
                    last = pe.matmul(ps[0][:, bank, width * a:width * (a + 1)],
                                     geo_sb[:, G_SUM + 128 * n:G_SUM + 128 * (n + 1)], rhs,
                                     start=(n == 0), stop=(n == len(SUM_PAIRS) - 1))
                last.then_inc(sum_done, 1)

            eye = geo_sb[:, G_EYE:G_EYE + 128]

            def transpose_block(pixels, shifted):
                for j in range(CHUNKS):
                    last = pe.transpose(pixels[:, j // 4, 128 * (j % 4):128 * (j % 4 + 1)],
                                        shifted[:, 128 * j:128 * (j + 1)], eye)
                return last

            def convolve_block(sums, pixels, weights):
                for bank in range(2):
                    seen = 16 * bank
                    for j in range(3 * bank, 3 * bank + 5):
                        lo = max(4 * j - 1, 16 * bank)
                        hi = min(4 * j + 5, 16 * bank + 16)
                        for a, b in ((lo, seen), (seen, hi)):
                            if a < b:
                                last = pe.matmul(sums[:, bank, 32 * (a - 16 * bank):32 * (b - 16 * bank)],
                                                 pixels[:, j, :], weights[:, a - (4 * j - 1):b - (4 * j - 1), :],
                                                 start=(j == 3 * bank), stop=(j == 3 * bank + 4 and b == hi))
                        seen = hi
                return last

            def transposes(k):
                if k < EARLY:
                    pe.wait_ge(shift_in[k], 16)
                else:
                    pe.wait_ge(centred, k - EARLY + 1)
                if k >= 2:
                    pe.wait_ge(flip_masked, k - 1)
                transpose_block(ps[k % 2], blk[:, DEEP + k % DEEP, :]).then_inc(flipped, 1)

            def convolve(k):
                pe.wait_ge(flip_masked, k + 1)
                if 2 <= k < 2 + EARLY:
                    pe.wait_ge(partial_done, k - 1)
                elif k >= 2:
                    pe.wait_ge(x1_done, k - 1)
                convolve_block(ps[2 + k % 2], flip[:, k % 2], conv_w[:, k]).then_inc(convolved, 1)

            pe.wait_ge(conv_w_done, 1)
            for k in range(EARLY):
                transposes(k)
            for k in range(EARLY):
                convolve(k)
            group_sums(1, 0, lambda b: stat[:, b, :, 0])
            group_sums(2, 1, lambda b: moment[:, b, 1, :])
            pe.wait_ge(gn_done, 1)
            transposes(EARLY)
            for k in range(EARLY, FAST):
                if k + 1 < FAST:
                    transposes(k + 1)
                convolve(k)

            pe.wait_ge(rank_done, 1)
            active = pe.value_load(count_i[0:1, 0:1], min_val=0, max_val=OFFSETS)
            with pe.If(active > FAST):
                pe.wait_ge(x1_done, FAST)
                with pe.Fori(FAST, OFFSETS) as k:
                    m = k - FAST
                    pe.wait_ge(more_centred, m + 1)
                    transpose_block(ps[0], blk[:, DEEP, :]).then_inc(more_flipped, 1)
                    pe.wait_ge(more_masked, m + 1)
                    pe.wait_ge(more_conv_w, m + 1)
                    convolve_block(ps[2], flip[:, 1], conv_w[:, 0]).then_inc(more_convolved, 1)

            group_sums(3, 0, lambda b: moment[:, b, :, :].rearrange("p k b -> p (k b)"))
            operands = (((2, 0), (0, 0)), ((2, 1), (0, 0)), ((2, 0), (1, 0)))
            for n in range(BATCH):
                for m in range(CT):
                    if CT * n + m >= 4:
                        pe.wait_ge(result_done, CT * n + m - 3)
                    sums = ps[(CT * n + m) % 4]
                    for at, (s, sign) in enumerate(operands[m]):
                        pe.wait_ge(low_done[s], n + 1)
                        for h in range(2):
                            for part in range(2):
                                last = pe.matmul(sums[:, h, :], had_sb[:, sign, :],
                                                 parts[:, n % 2, part, s, 512 * h:512 * (h + 1)],
                                                 start=(at == 0 and part == 0), stop=(at == 1 and part == 1))
                    last.then_inc(product_done, 1)

        @block.vector
        def _(dve):
            links = [0]

            def link(ins):
                links[0] += 1
                ins.then_inc(dve_link, 1)
                dve.wait_ge(dve_link, links[0])

            dve.wait_ge(const_in, 48)
            iota = geo_sb[:, G_IOTA:G_IOTA + OFFSETS]
            off_v = off_sb[:, :].rearrange("p (f k) -> p k f", k=2)
            o, rnd = wk[:, 0:2, :], px[:, 1:3, :]
            link(dve.tensor_scalar(o, off_v, PX_SCALE, 64.0, ALU.mult, ALU.min))
            link(dve.tensor_scalar(o, o, -64.0, None, ALU.max))
            link(dve.tensor_scalar(wk[:, 2:4, :], o, ROUND, None, ALU.add))
            link(dve.tensor_scalar(rnd, wk[:, 2:4, :], ROUND, None, ALU.subtract))
            link(dve.tensor_tensor(px[:, 3:5, :], o, rnd, ALU.subtract))
            dve.tensor_copy(px[:, 0, :], iota)
            link(dve.tensor_tensor(wk[:, 4:6, :], rnd, rnd, ALU.mult))
            link(dve.tensor_scalar(wk[:, 4:6, :], wk[:, 4:6, :], FAR * FAR, None, ALU.is_lt))
            link(dve.tensor_tensor(wk[:, 0, :], wk[:, 4, :], wk[:, 5, :], ALU.mult))
            link(dve.tensor_reduce(count_f[:, :], wk[:, 0, :], AX.X, ALU.add))
            dve.tensor_copy(count_i[:, :], count_f[:, :])
            link(dve.scalar_tensor_tensor(wk[:, 1, :], wk[:, 0, :], -float(OFFSETS), iota, ALU.mult, ALU.add))
            wide_v = wide.rearrange("p (f g) -> p f g", f=OFFSETS)
            full = [128, OFFSETS, OFFSETS]
            link(dve.tensor_tensor(wide_v, bc(wk[:, 1:2, :], full),
                                   bc(wk[:, 1, :].rearrange("p (f o) -> p f o", o=1), full), ALU.is_lt))
            link(dve.tensor_reduce(rank[:, :], wide_v, AX.X, ALU.add))

            link(dve.tensor_scalar(wk[:, 0, :], rank[:, :], float(BIND), None, ALU.mult))
            link(dve.tensor_reduce(wk[:, 1, 0:CLUSTERS], wk[:, 0, :].rearrange("p (a b) -> p a b", b=CLUSTER), AX.X, ALU.min))
            dve.tensor_copy(rows[:, 0:OFFSETS], wk[:, 0, :])
            dve.tensor_copy(rows[:, OFFSETS:], wk[:, 1, 0:CLUSTERS]).then_inc(rank_done, 1)

            def slot_parameters(slot_ids, n, link, placed, exp_in, exp_done, exp_count, weighed):
                keep = slice(0, n)
                shape = [128, n, OFFSETS]
                hit = wide[:, 0:n * OFFSETS].rearrange("p (k f) -> p k f", k=n)
                pick = wide[:, n * OFFSETS:2 * n * OFFSETS].rearrange("p (k f) -> p k f", k=n)
                rank_v = rank[:, :].rearrange("p (o f) -> p o f", o=1)
                link(dve.tensor_tensor(hit, bc(rank_v, shape), bc(slot_ids, shape), ALU.is_equal))
                for v in range(5):
                    link(dve.tensor_tensor(pick, hit, bc(px[:, v:v + 1, :], shape), ALU.mult))
                    link(dve.tensor_reduce(sel[:, keep, v], pick, AX.X, ALU.add))
                f, dx, dy = sel[:, keep, 0:1], sel[:, keep, 1:2], sel[:, keep, 2:3]
                link(dve.tensor_scalar(place_f[:, keep, 0:1], f, float(BIND), None, ALU.mult))
                link(dve.tensor_scalar(place_f[:, keep, 1:2], f, float(BIND * PIXELS), float(PIXELS), ALU.mult, ALU.add))
                link(dve.scalar_tensor_tensor(place_f[:, keep, 2:3], dy, -float(WIDTH), dx, ALU.mult, ALU.subtract))
                link(dve.tensor_scalar(place_f[:, keep, 2:3], place_f[:, keep, 2:3], 1.0 - PIXELS, PIXELS - 1.0, ALU.max, ALU.min))
                link(dve.tensor_tensor(place_f[:, keep, 2:3], place_f[:, keep, 2:3], place_f[:, keep, 1:2], ALU.add))
                dve.tensor_copy(place[:, keep, :], place_f[:, keep, :]).then_inc(placed, 1)
                link(dve.tensor_tensor(taps[:, keep, 0:35], bc(geo_sb[:, G_DX:G_DX + 35].rearrange("p (o d) -> p o d", o=1), [128, n, 35]),
                                       bc(sel[:, keep, 3:4], [128, n, 35]), ALU.add))
                link(dve.tensor_tensor(taps[:, keep, 35:44], bc(geo_sb[:, G_DY:G_DY + 9].rearrange("p (o d) -> p o d", o=1), [128, n, 9]),
                                       bc(sel[:, keep, 4:5], [128, n, 9]), ALU.add))
                dve.tensor_tensor(taps[:, keep, :], taps[:, keep, :], taps[:, keep, :], ALU.mult).then_inc(exp_in, 1)
                link(dve.tensor_tensor(view[:, keep, 0:CHUNKS], bc(geo_sb[:, G_ROW:G_ROW + CHUNKS].rearrange("p (o d) -> p o d", o=1), [128, n, CHUNKS]),
                                       bc(dy, [128, n, CHUNKS]), ALU.subtract))
                link(dve.tensor_tensor(view[:, keep, CHUNKS:], bc(geo_sb[:, G_COL:G_COL + 1].rearrange("p (o d) -> p o d", o=1), [128, n, 1]),
                                       dx, ALU.subtract))
                link(dve.tensor_scalar(view[:, keep, :], view[:, keep, :], 15.5, None, ALU.subtract))
                link(dve.tensor_tensor(view[:, keep, :], view[:, keep, :], view[:, keep, :], ALU.mult))
                link(dve.tensor_scalar(view[:, keep, :], view[:, keep, :], 256.0, None, ALU.is_lt))
                link(dve.tensor_tensor(view[:, keep, 0:CHUNKS], view[:, keep, 0:CHUNKS], bc(view[:, keep, CHUNKS:], [128, n, CHUNKS]), ALU.mult))
                dve.wait_ge(exp_done, exp_count)
                link(dve.tensor_tensor(taps[:, keep, :], taps[:, keep, :],
                                       bc(geo_sb[:, G_NEAR:G_NEAR + 44].rearrange("p (o d) -> p o d", o=1), [128, n, 44]), ALU.mult))
                link(dve.tensor_reduce(norm[:, keep, 0:1], taps[:, keep, 32:35], AX.X, ALU.add))
                link(dve.tensor_reduce(norm[:, keep, 1:2], taps[:, keep, 41:44], AX.X, ALU.add))
                link(dve.reciprocal(norm[:, keep, :], norm[:, keep, :]))
                link(dve.tensor_tensor(taps[:, keep, 0:32], taps[:, keep, 0:32], bc(norm[:, keep, 0:1], [128, n, 32]), ALU.mult))
                link(dve.tensor_tensor(taps[:, keep, 35:41], taps[:, keep, 35:41], bc(norm[:, keep, 1:2], [128, n, 6]), ALU.mult))
                link(dve.tensor_tensor(conv_w[:, keep, :, :],
                                       bc(taps[:, keep, 35:41].rearrange("p k (y o) -> p k y o", o=1), [128, n, 6, 32]),
                                       bc(taps[:, keep, 0:32].rearrange("p k (o x) -> p k o x", o=1), [128, n, 6, 32]), ALU.mult))
                dve.tensor_copy(norm[:, keep, :], norm[:, keep, :]).then_inc(weighed, 1)

            def slot_ids(k, n):
                return geo_sb[:, ds(G_IOTA + k, n)].rearrange("p (k o) -> p k o", o=1)

            slot_parameters(slot_ids(0, FAST), FAST, link, place_done, exp_in, exp_done, 1, conv_w_done)

            def combine(i):
                dve.wait_ge(stat_done, i + 1)
                for t in range(CT - 1):
                    last = dve.bn_aggr(stat[:, t, i, :], halfstat[:, i % 4, t, :, :].rearrange("p h s -> p (h s)"))
                return last

            for i in range(BATCH):
                dve.wait_ge(load_done[i % 4], 16 * (i // 4 + 1))
                for t in range(CT - 1):
                    for h in range(2):
                        last = dve.bn_stats(halfstat[:, i % 4, t, h, :], ring[:, t, place_of(i), 512 * h:512 * (h + 1)])
                last.then_inc(stat_done, 1)
                if i >= 1:
                    combine(i - 1)
            link(combine(BATCH - 1))
            dve.wait_ge(sum_stat_done, BATCH)
            deviation, second_moment = tmp[:, 1, 0, :], tmp[:, 2, 0, :]
            link(dve.tensor_scalar(deviation, sums[:, 0, :], 1.0 / PIXELS, None, ALU.mult))
            dve.tensor_tensor(stat[:, CT - 1, :, 0], pivot[:, :], deviation, ALU.subtract)
            link(dve.tensor_tensor(second_moment, deviation, deviation, ALU.mult))
            link(dve.scalar_tensor_tensor(stat[:, CT - 1, :, 1], sums[:, 1, :], 1.0 / PIXELS, second_moment, ALU.mult, ALU.subtract))

            def early_shares():
                keep, shape = slice(0, EARLY), [128, EARLY, 2, WIDTH]
                wide_shape = [128, EARLY, 2, WIDTH + 2]

                def const(at):
                    return bc(geo_sb[:, at:at + WIDTH + 2].rearrange("p (k a c) -> p k a c", k=1, a=1), wide_shape)
                link(dve.tensor_tensor(in_view, const(G_SPAN), bc(sel[:, keep, 1:3].rearrange("p k (a o) -> p k a o", o=1), wide_shape), ALU.subtract))
                link(dve.tensor_scalar(in_view, in_view, 15.5, None, ALU.subtract))
                link(dve.tensor_tensor(in_view, in_view, in_view, ALU.mult))
                link(dve.tensor_scalar(in_view, in_view, 256.0, None, ALU.is_lt))
                dve.tensor_tensor(tap3[:, :, 0, :], taps[:, keep, 32:35], bc(norm[:, keep, 0:1], [128, EARLY, 3]), ALU.mult)
                dve.tensor_tensor(tap3[:, :, 1, :], taps[:, keep, 41:44], bc(norm[:, keep, 1:2], [128, EARLY, 3]), ALU.mult)
                link(dve.tensor_tensor(in_view, in_view, const(G_INSIDE), ALU.mult))
                for d in range(3):
                    link(dve.tensor_tensor(product if d else share, in_view[:, :, :, d:d + WIDTH], bc(tap3[:, :, :, d:d + 1], shape), ALU.mult))
                    if d:
                        link(dve.tensor_tensor(share, share, product, ALU.add))

            mean, var = stat[:, :, :, 0], stat[:, :, :, 1]
            group_mean, variance, rstd = (tmp[:, n, :, :] for n in range(3))
            first_moment, second_moment = moment[:, :, 0, :], moment[:, :, 1, :]

            def centre_moments():
                link(dve.tensor_tensor(first_moment, mean, group_mean, ALU.subtract))
                link(dve.tensor_tensor(second_moment, first_moment, first_moment, ALU.mult))
                dve.tensor_tensor(second_moment, second_moment, var, ALU.add).then_inc(sum_in, 1)

            dve.memset(scrap[:, 0:1], 0.0).then_inc(sum_in, 1)
            early_shares()
            dve.wait_ge(sum_done, 1)
            by_tile = [ps[0][:, bank, 0:CT * BATCH].rearrange("p (t b) -> p t b", t=CT) for bank in range(2)]
            link(dve.tensor_scalar(group_mean, by_tile[0], 1.0 / GROUP, None, ALU.mult))
            centre_moments()
            dve.wait_ge(sum_done, 2)
            dve.tensor_scalar(variance, by_tile[1], 1.0 / GROUP, EPS, ALU.mult, ALU.add).then_inc(std_in, 1)
            dve.tensor_scalar(gn[:, :, :, 0], group_mean, -1.0, None, ALU.mult)
            dve.wait_ge(std_done, 1)
            link(dve.reciprocal(gn[:, :, :, 1], variance))
            dve.memset(scrap[:, 1:2], 0.0).then_inc(gn_done, 1)

            def mask_pixels(pixels, shifted, k):
                return dve.tensor_tensor(pixels, shifted[:, :, :].rearrange("p a (j c) -> p (a j) c", c=128),
                                         bc(view[:, k, 0:CHUNKS].rearrange("p (j o) -> p j o", o=1), [128, CHUNKS, 128]), ALU.mult)

            def add_displaced(x1, sums, rstd):
                return dve.scalar_tensor_tensor(x1, sums[:, :, :].rearrange("p a n -> p (a n)"), rstd, x1, ALU.mult, ALU.add)

            def mask_block(k):
                dve.wait_ge(flipped, k + 1)
                if k >= 2:
                    dve.wait_ge(convolved, k - 1)
                mask_pixels(flip[:, k % 2], ps[k % 2], k).then_inc(flip_masked, 1)

            def partial(k):
                u = k % DEEP
                dve.wait_ge(convolved, k + 1)
                dve.wait_ge(x_in[u], 16 * (k // DEEP + 1))
                return add_displaced(blk[:, u, :], ps[2 + k % 2], blk_gn[:, k, 1:2])

            def finish(k):
                u = k % DEEP
                dve.wait_ge(x1_done, k + 1)
                for h in range(2):
                    last = dve.bn_stats(blk_half[:, u, h, :], blk[:, u, 512 * h:512 * (h + 1)])
                link(last)
                dve.bn_aggr(blk_stat[:, u, :], blk_half[:, u, :, :].rearrange("p h s -> p (h s)")).then_inc(blk_stat_done, 1)

            for k in range(EARLY):
                dve.wait_ge(gn_in[k], 16)
                dve.tensor_scalar(share[:, k, 0, :], share[:, k, 0, :], blk_gn[:, k, 0:1], blk_gn[:, k, 1:2],
                                  ALU.mult, ALU.mult).then_inc(slope_ready, 1)
                partial(k).then_inc(partial_done, 1)
            mask_block(EARLY)
            for k in range(EARLY):
                dve.wait_ge(mean_share, k + 1)
                dve.wait_ge(partial_done, k + 1)
                dve.tensor_tensor(blk[:, k, :], blk[:, k, :], aside[k], ALU.add).then_inc(x1_done, 1)
                finish(k)
                if k == 0:
                    mask_block(EARLY + 1)
            for k in range(EARLY, FAST):
                if EARLY + 1 < k + 1 < FAST:
                    mask_block(k + 1)
                partial(k).then_inc(x1_done, 1)
                finish(k)

            active = dve.value_load(count_i[0:1, 0:1], min_val=0, max_val=OFFSETS)
            with dve.If(active > FAST):
                dve.wait_ge(convolved, FAST)
                for u in range(DEEP):
                    dve.wait_ge(blk_out[u], 32 * blocks_in(u))
                with dve.Fori(FAST, OFFSETS) as k:
                    m = k - FAST
                    step = [0]

                    def more(ins):
                        step[0] += 1
                        ins.then_inc(more_link, 1)
                        dve.wait_ge(more_link, MORE_LINKS * m + step[0])

                    slot_parameters(slot_ids(k, 1), 1, more, more_placed, more_exp_in, more_exp_done, m + 1, more_conv_w)
                    dve.wait_ge(more_flipped, m + 1)
                    mask_pixels(flip[:, 1], ps[0], 0).then_inc(more_masked, 1)
                    dve.wait_ge(more_convolved, m + 1)
                    more(add_displaced(blk[:, 0, :], ps[2], blk_gn[:, 0, 1:2]))
                    for h in range(2):
                        last = dve.bn_stats(blk_half[:, 0, h, :], blk[:, 0, 512 * h:512 * (h + 1)])
                    more(last)
                    dve.memset(scrap[:, 2:3], 0.0)
                    dve.bn_aggr(blk_stat[:, 0, :], blk_half[:, 0, :, :].rearrange("p h s -> p (h s)")).then_inc(more_ready, 1)
                    dve.wait_ge(more_out, 32 * m + 32)
                    dve.memset(scrap[:, 3:4], 0.0)
                    assert step[0] == MORE_LINKS, step[0]

            dve.wait_ge(stat_patched, 16)
            centre_moments()
            dve.wait_ge(sum_done, 3)
            by_tile = ps[0][:, 0, 0:2 * CT * BATCH].rearrange("p (t k b) -> p t k b", t=CT, k=2)
            shift, square = rstd, first_moment
            link(dve.tensor_scalar(shift, by_tile[:, :, 0, :], 1.0 / GROUP, None, ALU.mult))
            dve.tensor_scalar(variance, by_tile[:, :, 1, :], 1.0 / GROUP, EPS, ALU.mult, ALU.add)
            link(dve.tensor_tensor(square, shift, shift, ALU.mult))
            dve.tensor_tensor(variance, variance, square, ALU.subtract).then_inc(std_in, 1)
            link(dve.tensor_tensor(group_mean, group_mean, shift, ALU.add))
            dve.wait_ge(std_done, 2)
            link(dve.reciprocal(rstd, variance))
            scale, bias = gn[:, :, :, 0], gn[:, :, :, 1]
            link(dve.tensor_scalar(scale, rstd, HALF_SCALE, None, ALU.mult))
            dve.scalar_tensor_tensor(bias, group_mean, -1.0, scale, ALU.mult, ALU.mult).then_inc(gn_done, 1)

            def result(n, m):
                i = n + EXTRA
                dve.wait_ge(product_done, CT * n + m + 1)
                dve.scalar_tensor_tensor(ring[:, m, place_of(i), :], ps[(CT * n + m) % 4][:, :, :].rearrange("p a n -> p (a n)"),
                                         1.0 / (HALF_SCALE * float(np.sqrt(TARGET))), ring[:, m, place_of(i), :],
                                         ALU.mult, ALU.add).then_inc(result_done, 1)

            mix_a(dve, 0)
            mix_b(dve, 0)
            low(dve, 0, 2, middle)
            low(dve, 0, 0, sum_a(0))
            low(dve, 0, 1, last_tile(0))
            low(dve, 1, 2, middle)
            for m in range(CT):
                result(0, m)
            for n in range(1, BATCH):
                low(dve, n, 0, sum_a(n))
                if n >= 2:
                    result(n - 1, 1)
                low(dve, n, 1, last_tile(n))
                if n >= 2:
                    result(n - 1, 2)
                if n + 1 < BATCH and n + 1 not in POOL_LOW:
                    low(dve, n + 1, 2, middle)
                result(n, 0)
            for m in range(1, CT):
                result(BATCH - 1, m)


def kernel(x, L0_conv_offset):
    import concourse.bacc as bacc
    from concourse.bass_utils import run_bass_kernel_spmd

    x = np.ascontiguousarray(x)
    x_pad = np.zeros((BATCH, (CHANNELS + 2) * PIXELS), x.dtype)
    x_pad[:, PIXELS:PIXELS * (CHANNELS + 1)] = x.reshape(BATCH, -1)
    arrays = {"x_pad": x_pad, "offset": np.ascontiguousarray(L0_conv_offset),
              "geo": geometry_constants(), "had": hadamard_constants()}
    nc = bacc.Bacc("TRN2", target_bir_lowering=False, num_devices=1)
    args = [nc.dram_tensor(name, a.shape, mybir.dt.from_np(a.dtype), kind="ExternalInput").ap() for name, a in arrays.items()]
    out = nc.dram_tensor("out", (BATCH, CHANNELS, HEIGHT, WIDTH), FP32, kind="ExternalOutput").ap()
    build(nc, *args, out)
    r = run_bass_kernel_spmd(nc, [arrays], core_ids=[0])
    return r.results[0]["out"]
```
